# Optimizing a Trainium2 kernel written in Bass

```python
import numpy as np
import jax
import jax.numpy as jnp

def _softmax(x, axis=-1):
    return jax.nn.softmax(x, axis=axis)

def _gelu(x):
    return jax.nn.gelu(x, approximate=True)

def _silu(x):
    return jax.nn.silu(x)

def _sigmoid(x):
    return jax.nn.sigmoid(x)

def _layernorm(x, axis=-1, eps=1e-05):
    m = jnp.mean(x, axis=axis, keepdims=True)
    v = jnp.var(x, axis=axis, keepdims=True)
    return (x - m) / jnp.sqrt(v + eps)

def _scatter_add(tgt, idx, src, axis=0):
    return tgt.at[idx].add(src)

def _segment_sum(src, seg, n):
    return jax.ops.segment_sum(src, seg, n)
kernel_name = 'mk_sandwich_d1_jaxref_r8_5a9215'

def setup_inputs(seed: int=0):
    np.random.seed(seed)
    _w = jnp.asarray

    def _L0_attn_setup():
        import jax, jax.numpy as jnp
        import numpy as np
        NUM_HEADS = 16
        WINDOW_SIZE = 32
        key = jax.random.key(seed)
        ks = jax.random.split(key, 5)
        B, S, H = (2, 256, 128)
        scale = 0.02
        return {'x': jax.random.normal(ks[0], (B, S, H), dtype=jnp.float32), 'Wq': jax.random.normal(ks[1], (H, H), dtype=jnp.float32) * scale, 'bq': jnp.zeros((H,), dtype=jnp.float32), 'Wk': jax.random.normal(ks[2], (H, H), dtype=jnp.float32) * scale, 'bk': jnp.zeros((H,), dtype=jnp.float32), 'Wv': jax.random.normal(ks[3], (H, H), dtype=jnp.float32) * scale, 'bv': jnp.zeros((H,), dtype=jnp.float32), 'Wo': jax.random.normal(ks[4], (H, H), dtype=jnp.float32) * scale, 'bo': jnp.zeros((H,), dtype=jnp.float32)}
    _L0_attn_in = _L0_attn_setup()

    def _L0_ffn_setup():
        import jax, jax.numpy as jnp
        import numpy as np
        B, S, H = (2, 256, 128)
        I = 64
        E_R, E_Z = (32, 8)
        E_T = E_R + E_Z
        K = 6
        SCALE = 2.5
        W_INIT = 0.02
        key = jax.random.key(seed)
        k0, k1, k2, k3 = jax.random.split(key, 4)
        return {'hidden_states': jax.random.normal(k0, (B, S, H), jnp.float32), 'classifier_weight': jax.random.normal(k1, (E_T, H), jnp.float32) * W_INIT, 'e_score_correction_bias': jnp.zeros((E_T,), jnp.float32), 'gate_up_proj': jax.random.normal(k2, (E_T, 2 * I, H), jnp.float32) * W_INIT, 'down_proj': jax.random.normal(k3, (E_R, H, I), jnp.float32) * W_INIT}
    _L0_ffn_in = _L0_ffn_setup()
    _d = {'L0_attn_x': _L0_attn_in['x'], 'L0_attn_Wq': _L0_attn_in['Wq'], 'L0_attn_bq': _L0_attn_in['bq'], 'L0_attn_Wk': _L0_attn_in['Wk'], 'L0_attn_bk': _L0_attn_in['bk'], 'L0_attn_Wv': _L0_attn_in['Wv'], 'L0_attn_bv': _L0_attn_in['bv'], 'L0_attn_Wo': _L0_attn_in['Wo'], 'L0_attn_bo': _L0_attn_in['bo'], 'L0_ffn_classifier_weight': _L0_ffn_in['classifier_weight'], 'L0_ffn_e_score_correction_bias': _L0_ffn_in['e_score_correction_bias'], 'L0_ffn_gate_up_proj': _L0_ffn_in['gate_up_proj'], 'L0_ffn_down_proj': _L0_ffn_in['down_proj']}
    _x0 = _d['L0_attn_x']
    _d['L0_attn_x'] = jax.random.normal(jax.random.fold_in(jax.random.key(seed), 1), (4, 512, 128), dtype=_x0.dtype)
    del _x0
    return _d

def reference(L0_attn_x, L0_attn_Wq, L0_attn_bq, L0_attn_Wk, L0_attn_bk, L0_attn_Wv, L0_attn_bv, L0_attn_Wo, L0_attn_bo, L0_ffn_classifier_weight, L0_ffn_e_score_correction_bias, L0_ffn_gate_up_proj, L0_ffn_down_proj):

    def _L0_attn_ref(x, Wq, bq, Wk, bk, Wv, bv, Wo, bo):
        import jax, jax.numpy as jnp
        import numpy as np
        NUM_HEADS = 16
        WINDOW_SIZE = 32
        B, S, Hs = x.shape
        nh = NUM_HEADS
        hd = Hs // nh
        half_w = WINDOW_SIZE // 2
        q = (x @ Wq + bq).reshape(B, S, nh, hd)
        k = (x @ Wk + bk).reshape(B, S, nh, hd)
        v = (x @ Wv + bv).reshape(B, S, nh, hd)
        scores = jnp.einsum('bqhd,bkhd->bhqk', q, k) / jnp.sqrt(jnp.asarray(hd, x.dtype))
        idx = jnp.arange(S)
        band = jnp.abs(idx[:, None] - idx[None, :]) <= half_w
        scores = jnp.where(band[None, None, :, :], scores, -jnp.inf)
        attn = jax.nn.softmax(scores, axis=-1)
        out = jnp.einsum('bhqk,bkhd->bqhd', attn, v).reshape(B, S, Hs)
        return out @ Wo + bo

    def _L0_ffn_ref(hidden_states, classifier_weight, e_score_correction_bias, gate_up_proj, down_proj):
        import jax, jax.numpy as jnp
        import numpy as np
        B, S, H = (2, 256, 128)
        I = 64
        E_R, E_Z = (32, 8)
        E_T = E_R + E_Z
        K = 6
        SCALE = 2.5
        W_INIT = 0.02
        orig_shape = hidden_states.shape
        x = hidden_states.reshape(-1, H).astype(jnp.float32)
        T = x.shape[0]
        logits = x @ classifier_weight.T
        scores = jax.nn.softmax(logits, axis=-1)
        _, topk_idx = jax.lax.top_k(scores + e_score_correction_bias[None, :], K)
        topk_w = jnp.take_along_axis(scores, topk_idx, axis=1) * SCALE
        w_full = jnp.zeros((T, E_T), jnp.float32).at[jnp.arange(T)[:, None], topk_idx].add(topk_w)
        zero_w = w_full[:, E_R:].sum(axis=-1, keepdims=True)
        out0 = x * zero_w
        routed_w = w_full[:, :E_R].T

        def body(out, xs):
            Wgu, Wd, we = xs
            gate, up = jnp.split(x @ Wgu.T, 2, axis=-1)
            y = jax.nn.silu(gate) * up @ Wd.T
            return (out + we[:, None] * y, None)
        out, _ = jax.lax.scan(body, out0, (gate_up_proj[:E_R], down_proj, routed_w))
        return out.reshape(orig_shape).astype(hidden_states.dtype)
    x = L0_attn_x
    x = x + _layernorm(_L0_attn_ref(_layernorm(x, axis=-1), L0_attn_Wq, L0_attn_bq, L0_attn_Wk, L0_attn_bk, L0_attn_Wv, L0_attn_bv, L0_attn_Wo, L0_attn_bo), axis=-1)
    x = x + _layernorm(_L0_ffn_ref(_layernorm(x, axis=-1), L0_ffn_classifier_weight, L0_ffn_e_score_correction_bias, L0_ffn_gate_up_proj, L0_ffn_down_proj), axis=-1)
    return x

_drawn_inputs = setup_inputs


def setup_inputs(seed=0):
    import zlib

    import numpy as np

    out = dict(_drawn_inputs(seed))
    spreads = {'L0_attn_bq': (0.0, 0.8),
     'L0_attn_bk': (0.0, 0.8),
     'L0_attn_bv': (0.0, 0.1),
     'L0_attn_bo': (0.0, 0.1),
     'L0_ffn_e_score_correction_bias': (0.0, 0.1)}
    factors = {'L0_attn_Wq': 8.0,
     'L0_attn_Wk': 8.0,
     'L0_ffn_classifier_weight': 8.0,
     'L0_ffn_gate_up_proj': 8.0,
     'L0_ffn_down_proj': 8.0}
    for name, (base, spread) in spreads.items():
        noise = np.random.default_rng([zlib.crc32(name.encode()), seed]).standard_normal(out[name].shape)
        drawn = base * np.exp(spread * noise) if base else spread * noise
        out[name] = jnp.asarray(drawn.astype(out[name].dtype))
    for name, factor in factors.items():
        out[name] = (out[name] * factor).astype(out[name].dtype)
    return out
```

```python
from contextlib import ExitStack

import numpy as np

import concourse.bass as bass
from concourse import mybir
from concourse.alu_op_type import AluOpType as ALU

ACT = mybir.ActivationFunctionType
F32 = mybir.dt.float32
F32R = mybir.dt.float32r
BF16 = mybir.dt.bfloat16
AX_X = mybir.AxisListType.X

P = 128
HEADS, HD = 16, 8
HG = 4
HPG = HEADS // HG
HALF_W = 16
QB = 32
KW = QB + 2 * HALF_W
NEG = -1e30
EPS = 1e-5
EXPERTS, ROUTED, TOPK = 40, 32, 6
PAIRS = ROUTED // 2
INNER = 64
ROUTE_SCALE = 2.5
TAKEN, SENTINEL = 3e38, -3e38


def shape_constants(S):
    nb = S // QB
    ident = np.eye(P, dtype=np.float32)
    p = np.arange(P)
    qmask = ((p[:, None] // HD) % HPG == np.arange(HPG)).astype(np.float32)
    vmask = (p[:, None] // QB == np.arange(HPG)).astype(np.float32)
    sel = np.zeros((P, PAIRS, P), np.float32)
    for pair in range(PAIRS):
        for m in range(P):
            e = 2 * pair + m // INNER
            sel[[e, ROUTED + e], pair, m] = 1.0
    table = np.concatenate([ident, qmask, vmask], axis=1)
    q = np.arange(P) % QB
    band = np.zeros((P, nb, KW), np.float32)
    for b in range(nb):
        query, key = b * QB + q[:, None], b * QB - HALF_W + np.arange(KW)[None, :]
        seen = (np.abs(query - key) <= HALF_W) & (key >= 0) & (key < S)
        band[:, b] = np.where(seen, 0.0, NEG)
    return table, band.reshape(P, nb * KW), sel[0:2 * ROUTED].reshape(2 * ROUTED, PAIRS * P)


def build_block(nc, x, Wq, bq, Wk, bk, Wv, bv, Wo, bo, cls_w, cls_bias, w_gu, w_down, table, band, selector, out):
    NSEQ, S, _ = x.shape
    TILES = S // P
    NB = S // QB
    NC = NB + 1
    PAD = HALF_W
    GW = HPG * HD + HPG
    HALF = NB // 2
    scale = 1.0 / float(np.sqrt(HD))
    TW = P + 2 * HPG

    with ExitStack() as ctx:
        def sb(name, shape, dt=F32):
            return ctx.enter_context(nc.sbuf_tensor(name, shape, dt))

        def sem(name):
            return ctx.enter_context(nc.semaphore(name))

        def bank(name):
            return ctx.enter_context(nc.psum_tensor(name, [P, 512], F32))
        gate_ps, up_ps, route_ps, y_ps = bank("gate_ps"), bank("up_ps"), bank("route_ps"), bank("y_ps")
        score_ps = ctx.enter_context(nc.psum_tensor("score_ps", [P, 2, 512], F32))
        work_a, work_b = bank("work_a"), bank("work_b")

        table_sb = sb("table_sb", [P, TW])
        ident = table_sb[:, 0:P]
        qmask = table_sb[:, P:P + HPG]
        vmask = table_sb[:, P + HPG:TW]
        ident_bf = sb("ident_bf", [P, P], BF16)
        select = sb("select", [2 * ROUTED, PAIRS * P], F32R)
        band_sb = sb("band_sb", [P, NB * KW])
        band_bf = sb("band_bf", [P, NB * KW], BF16)
        minus_half = sb("minus_half", [P, TILES])
        eps_sb = sb("eps_sb", [P, TILES])
        wq_sb, wk_sb, wv_sb, wo_sb = (sb(n, [P, P]) for n in ("wq_sb", "wk_sb", "wv_sb", "wo_sb"))
        bq_sb, bk_sb, bv_sb = (sb(n, [P, 1]) for n in ("bq_sb", "bk_sb", "bv_sb"))
        bq_masked = sb("bq_masked", [P, HPG])
        bv_wide = sb("bv_wide", [P, P])
        bo_wide = sb("bo_wide", [P, P])
        out_bias = sb("out_bias", [P, P])
        cls_sb = sb("cls_sb", [EXPERTS, P])
        cls_t = sb("cls_t", [P, EXPERTS])
        cls_bias_sb = sb("cls_bias_sb", [P, EXPERTS])
        gu_hi, gu_lo = (sb(n, [P, PAIRS, 2, P], F32R) for n in ("gu_hi", "gu_lo"))
        down_hi, down_lo = (sb(n, [P, PAIRS, P], F32R) for n in ("down_hi", "down_lo"))

        x_all = sb("x_all", [P, NSEQ * TILES, P])
        res_all = sb("res_all", [P, NSEQ * TILES, P])
        stats = sb("stats", [P, TILES, 6])
        moments = sb("moments", [P, TILES, 2])
        var_eps = sb("var_eps", [P, TILES])
        rstd = sb("rstd", [P, TILES])
        xn = sb("xn", [P, TILES, P])
        xn_t = sb("xn_t", [P, S + 2 * PAD])
        q_blocks = sb("q_blocks", [P, NB, HPG, QB])
        k_t = sb("k_t", [P, S + 2 * PAD])
        v_blocks = sb("v_blocks", [P, NC, HG, GW])
        row_max = sb("row_max", [P, 2, HALF])
        shifted = sb("shifted", [P, 2, 2 * HALF * KW])
        probs = sb("probs", [P, 2, 2 * HALF * KW])
        probs_t = sb("probs_t", [P, HG, NB * KW])
        denom_inv = sb("denom_inv", [P, TILES, HG, HPG])
        heads_out = sb("heads_out", [P, TILES, P])
        heads_t = sb("heads_t", [P, S])
        attn = sb("attn", [P, TILES, P])
        attn_n = sb("attn_n", [P, TILES, P])
        x1 = sb("x1", [P, TILES, P])
        x2 = sb("x2", [P, TILES, P])
        x2_t = sb("x2_t", [P, S])
        x2_hi, x2_lo = sb("x2_hi", [P, S], F32R), sb("x2_lo", [P, S], F32R)
        r_max = sb("r_max", [P, TILES])
        r_shift = sb("r_shift", [P, TILES, EXPERTS])
        r_exp = sb("r_exp", [P, TILES, EXPERTS])
        r_sum = sb("r_sum", [P, TILES])
        r_inv = sb("r_inv", [P, TILES])
        r_score = sb("r_score", [P, TILES, EXPERTS])
        r_biased = sb("r_biased", [P, TILES, EXPERTS + 2])
        top8 = sb("top8", [P, TILES, 8])
        r_marked = sb("r_marked", [P, TILES, EXPERTS + 2])
        r_scaled = sb("r_scaled", [P, TILES, EXPERTS])
        r_weight = sb("r_weight", [P, TILES, EXPERTS])
        zero_w = sb("zero_w", [P, TILES])
        route_hl = sb("route_hl", [P, TILES, P], F32R)
        route_t = sb("route_t", [2 * ROUTED, S], F32R)
        silu_sb = sb("silu_sb", [P, 2, S])
        gated = sb("gated", [P, 2, S])
        hidden = sb("hidden", [P, 2, S])
        h_hi, h_lo = sb("h_hi", [P, 3, S], F32R), sb("h_lo", [P, 3, S], F32R)
        y_t = sb("y_t", [P, S])
        ffn = sb("ffn", [P, TILES, P])
        ffn_n = sb("ffn_n", [P, TILES, P])

        gu_rows = probs_t[:].rearrange("p g c -> p (g c)").rearrange("p (a s m) -> p a s m", a=PAIRS, s=2)
        down_rows = probs[:].rearrange("p u c -> p (u c)").rearrange("p (a m) -> p a m", a=PAIRS)
        selector_rows = res_all[0:2 * ROUTED].rearrange("p t h -> p (t h)")

        consts_in, small_in, gu_in, down_in, x_in, out_done = map(sem, (
            "consts_in", "small_in", "gu_in", "down_in", "x_in", "out_done"))
        pool_consts = sem("pool_consts")
        tables_ready = sem("tables_ready")
        turned = sem("turned")
        turned_hi = sem("turned_hi")
        turned_lo = sem("turned_lo")
        setup_pe = sem("setup_pe")
        setup_act = sem("setup_act")
        blocks_zero = sem("blocks_zero")
        pads_set = sem("pads_set")
        dve_step = sem("dve_step")
        pool_step = sem("pool_step")
        moments_ready, rstd_ready = sem("moments_ready"), sem("rstd_ready")
        xn_ready, xn_turned, xn_t_ready = sem("xn_ready"), sem("xn_turned"), sem("xn_t_ready")
        q_done, k_done, q_ready, k_ready = sem("q_done"), sem("k_done"), sem("q_ready"), sem("k_ready")
        v_done, v_ready = sem("v_done"), sem("v_ready")
        scores_done, shifted_ready, probs_ready, probs_t_ready = map(sem, (
            "scores_done", "shifted_ready", "probs_ready", "probs_t_ready"))
        pv_done, heads_ready, heads_turned, heads_t_ready, attn_done = map(sem, (
            "pv_done", "heads_ready", "heads_turned", "heads_t_ready", "attn_done"))
        x2_ready, x2_turned, x2_t_ready, x2_hi_ready, x2_lo_ready = map(sem, (
            "x2_ready", "x2_turned", "x2_t_ready", "x2_hi_ready", "x2_lo_ready"))
        logits_done, r_shift_ready, r_exp_ready, route_ready, route_turned, route_t_ready = map(sem, (
            "logits_done", "r_shift_ready", "r_exp_ready", "route_ready", "route_turned", "route_t_ready"))
        gate_done, up_done, route_wide, silu_ready, gated_ready, hidden_ready = map(sem, (
            "gate_done", "up_done", "route_wide", "silu_ready", "gated_ready", "hidden_ready"))
        h_hi_ready, h_lo_ready, down_done = map(sem, ("h_hi_ready", "h_lo_ready", "down_done"))
        y_t_ready, y_turned, res_ready = map(sem, ("y_t_ready", "y_turned", "res_ready"))

        GU_BANKS, DOWN_BANKS = 2 * PAIRS // 4, PAIRS // 4
        STAGES = [(gp, hf) for gp in range(HG // 2) for hf in range(2)]
        SMALL = 10

        block = ctx.enter_context(nc.Block())

        @block.sync
        def _(sp):
            sp.dma_start(x_all[:], x.rearrange("s (j p) h -> p (s j) h", p=P)).then_inc(x_in, 16)
            sp.dma_start(table_sb[:], table).then_inc(consts_in, 16)
            sp.dma_start(band_sb[:], band).then_inc(consts_in, 16)
            sp.dma_start(selector_rows, selector).then_inc(consts_in, 16)
            for dst, src in ((wq_sb, Wq), (wk_sb, Wk), (wv_sb, Wv), (wo_sb, Wo)):
                sp.dma_start(dst[:], src).then_inc(small_in, 16)
            for dst, src in ((bq_sb, bq), (bk_sb, bk), (bv_sb, bv)):
                sp.dma_start(dst[:], src.rearrange("(p a) -> p a", a=1)).then_inc(small_in, 16)
            sp.dma_start(bo_wide[:], bo.partition_broadcast(P)).then_inc(small_in, 16)
            sp.dma_start(cls_bias_sb[:], cls_bias.partition_broadcast(P)).then_inc(small_in, 16)
            sp.dma_start(cls_sb[:], cls_w).then_inc(small_in, 16)
            gu = w_gu[0:ROUTED].rearrange("(p e) (s i) h -> e i p s h", e=2, s=2)
            for e in range(2):
                for s in range(2):
                    sp.dma_start(gu_rows[INNER * e:INNER * (e + 1), :, s, :], gu[e, :, :, s, :]).then_inc(gu_in, 16)
            sp.dma_start(down_rows.rearrange("h p (e i) -> h (p e) i", e=2),
                         w_down.rearrange("e h i -> h e i")).then_inc(down_in, 16)
            with sp.Fori(0, NSEQ) as s:
                sp.wait_ge(res_ready, s + 1)
                sp.dma_start(out[bass.ds(s, 1)].rearrange("a (j p) h -> p (a j) h", p=P),
                             res_all[:, bass.ds(s * TILES, TILES), :]).then_inc(out_done, 16)
            sp.wait_ge(out_done, 16 * NSEQ)

        @block.gpsimd
        def _(pool):
            pool.memset(minus_half[:], -0.5).then_inc(pool_consts, 1)
            pool.memset(eps_sb[:], EPS).then_inc(pool_consts, 1)
            pool.memset(route_hl[:, :, 2 * ROUTED:].bitcast(F32), 0.0).then_inc(pool_consts, 1)
            pool.memset(r_biased[:], SENTINEL).then_inc(pool_consts, 1)
            pool.memset(v_blocks[:], 0.0).then_inc(blocks_zero, 1)
            for t in (xn_t, k_t):
                pool.memset(t[:, 0:PAD], 0.0).then_inc(pads_set, 1)
                pool.memset(t[:, S + PAD:S + 2 * PAD], 0.0).then_inc(pads_set, 1)
            pool.wait_ge(pool_consts, 4)

            def inverse_deviation(s, k):
                pool.wait_ge(moments_ready, s * 4 + k)
                pool.tensor_tensor(var_eps[:], moments[:, :, 1], eps_sb[:], ALU.add).then_inc(pool_step, 1)
                pool.wait_ge(pool_step, s * 4 + k)
                pool.tensor_tensor(rstd[:], var_eps[:], minus_half[:], ALU.pow).then_inc(rstd_ready, 1)

            def x2_low(s):
                pool.wait_ge(x2_t_ready, s + 1)
                pool.wait_ge(x2_hi_ready, s + 1)
                pool.tensor_tensor(x2_lo[:], x2_t[:], x2_hi[:].bitcast(F32), ALU.subtract).then_inc(x2_lo_ready, 1)

            def hidden_low(s, p):
                n = s * PAIRS + p
                pool.wait_ge(h_hi_ready, n + 1)
                if p >= 3:
                    pool.wait_ge(down_done, n - 2)
                pool.tensor_tensor(h_lo[:, p % 3, :], hidden[:, p % 2, :], h_hi[:, p % 3, :].bitcast(F32),
                                   ALU.subtract).then_inc(h_lo_ready, 1)

            with pool.Fori(0, NSEQ) as s:
                for k in (1, 2, 3):
                    inverse_deviation(s, k)
                x2_low(s)
                for p in range(PAIRS):
                    hidden_low(s, p)
                inverse_deviation(s, 4)

        @block.scalar
        def _(act):
            for n in range(GU_BANKS):
                act.wait_ge(turned, n + 1)
                act.activation(gu_hi[:, 2 * n:2 * n + 2].rearrange("p a s m -> p (a s m)"),
                               (work_a, work_b)[n % 2][:], ACT.Copy).then_inc(turned_hi, 1)
            for n in range(DOWN_BANKS):
                act.wait_ge(turned, GU_BANKS + n + 1)
                act.activation(down_hi[:, 4 * n:4 * n + 4].rearrange("p a m -> p (a m)"),
                               (work_a, work_b)[n % 2][:], ACT.Copy).then_inc(turned_hi, 1)
            act.wait_ge(tables_ready, 1)
            act.wait_ge(small_in, 16 * SMALL)
            act.wait_ge(pads_set, 4)

            def turn_xn(s):
                act.wait_ge(xn_turned, s + 1)
                act.activation(xn_t[:, PAD:PAD + S], work_a[:], ACT.Copy).then_inc(xn_t_ready, 1)

            def queries_keys(s):
                act.wait_ge(q_done, s + 1)
                for h in range(HPG):
                    act.activation(q_blocks[:, :, h, :], work_b[:].rearrange("p (b q) -> p b q", b=NB), ACT.Identity, bias=bq_masked[:, h:h + 1],
                                   scale=qmask[:, h:h + 1]).then_inc(q_ready, 1)
                act.wait_ge(k_done, s + 1)
                act.activation(k_t[:, PAD:PAD + S], work_a[:], ACT.Identity, bias=bk_sb[:, 0:1]).then_inc(k_ready, 1)

            def values(s):
                act.wait_ge(v_done, s + 1)
                for h in range(HPG):
                    keys = slice(QB * h, QB * (h + 1))
                    act.activation(v_blocks[keys, :, :, HD * h:HD * (h + 1)],
                                   score_ps[keys].rearrange("p a c -> p (a c)")[:, 0:NC * HG * HD].rearrange(
                                       "p (c g d) -> p c g d", c=NC, g=HG), ACT.Copy).then_inc(v_ready, 1)

            def exponentials(s, u):
                n = s * len(STAGES) + u
                act.wait_ge(shifted_ready, n + 1)
                if u >= 2:
                    act.wait_ge(probs_t_ready, n - 1)
                act.activation(probs[:, u % 2, :], shifted[:, u % 2, :], ACT.Exp, scale=scale).then_inc(probs_ready, 1)

            def turn_heads(s):
                act.wait_ge(heads_turned, s + 1)
                act.activation(heads_t[:], score_ps[:, 0, :], ACT.Copy).then_inc(heads_t_ready, 1)

            def turn_x2(s):
                act.wait_ge(x2_turned, s + 1)
                act.activation(x2_hi[:], work_a[:], ACT.Copy).then_inc(x2_hi_ready, 1)
                act.activation(x2_t[:], work_a[:], ACT.Copy).then_inc(x2_t_ready, 1)

            def route_exp(s):
                act.wait_ge(r_shift_ready, s + 1)
                act.activation(r_exp[:], r_shift[:], ACT.Exp).then_inc(r_exp_ready, 1)

            def turn_route(s):
                act.wait_ge(route_turned, s + 1)
                act.activation(route_t[:], work_a[0:2 * ROUTED, :], ACT.Copy).then_inc(route_t_ready, 1)

            def silu(s, p):
                n = s * PAIRS + p
                act.wait_ge(gate_done, n + 1)
                if p >= 2:
                    act.wait_ge(gated_ready, n - 1)
                act.activation(silu_sb[:, p % 2, :], gate_ps[:], ACT.Silu).then_inc(silu_ready, 1)

            def hidden_high(s, p):
                n = s * PAIRS + p
                act.wait_ge(hidden_ready, n + 1)
                if p >= 3:
                    act.wait_ge(down_done, n - 2)
                act.activation(h_hi[:, p % 3, :], hidden[:, p % 2, :], ACT.Copy).then_inc(h_hi_ready, 1)

            def take_y(s):
                act.wait_ge(down_done, (s + 1) * PAIRS)
                act.activation(y_t[:], y_ps[:], ACT.Copy).then_inc(y_t_ready, 1)

            with act.Fori(0, NSEQ) as s:
                turn_xn(s)
                queries_keys(s)
                values(s)
                for u in range(len(STAGES)):
                    exponentials(s, u)
                turn_heads(s)
                turn_x2(s)
                route_exp(s)
                turn_route(s)
                for p in range(PAIRS):
                    silu(s, p)
                    if p >= 1:
                        hidden_high(s, p - 1)
                hidden_high(s, PAIRS - 1)
                take_y(s)

        @block.vector
        def _(dve):
            steps = [0]

            def ordered(ins):
                steps[0] += 1
                ins.then_inc(dve_step, 1)
                dve.wait_ge(dve_step, steps[0])

            dve.wait_ge(x_in, 16)
            dve.wait_ge(consts_in, 48)
            dve.tensor_copy(ident_bf[:], ident).then_inc(tables_ready, 1)
            dve.tensor_copy(band_bf[:], band_sb[:]).then_inc(tables_ready, 1)
            dve.tensor_copy(select[:], selector_rows).then_inc(tables_ready, 1)
            dve.wait_ge(blocks_zero, 1)
            for h in range(HPG):
                dve.tensor_copy(v_blocks[:, :, :, HPG * HD + h],
                                vmask[:, h:h + 1].unsqueeze(1).broadcast_to([P, NC, HG])).then_inc(tables_ready, 1)
            dve.wait_ge(small_in, 16 * SMALL)
            dve.tensor_scalar(bq_masked[:], qmask, bq_sb[:, 0:1], None, ALU.mult).then_inc(tables_ready, 1)
            dve.tensor_copy(bv_wide[:], bv_sb[:, 0:1].broadcast_to([P, P])).then_inc(tables_ready, 1)
            for n in range(GU_BANKS):
                dve.wait_ge(turned_hi, n + 1)
                dve.tensor_tensor(gu_lo[:, 2 * n:2 * n + 2].rearrange("p a s m -> p (a s m)"),
                                  (work_a, work_b)[n % 2][:],
                                  gu_hi[:, 2 * n:2 * n + 2].rearrange("p a s m -> p (a s m)").bitcast(F32),
                                  ALU.subtract).then_inc(turned_lo, 1)
            for n in range(DOWN_BANKS):
                dve.wait_ge(turned_hi, GU_BANKS + n + 1)
                dve.tensor_tensor(down_lo[:, 4 * n:4 * n + 4].rearrange("p a m -> p (a m)"),
                                  (work_a, work_b)[n % 2][:],
                                  down_hi[:, 4 * n:4 * n + 4].rearrange("p a m -> p (a m)").bitcast(F32),
                                  ALU.subtract).then_inc(turned_lo, 1)
            dve.wait_ge(setup_pe, 1)
            dve.tensor_tensor(out_bias[:], score_ps[:, 0, 0:P], bo_wide[:], ALU.add).then_inc(setup_act, 1)
            dve.tensor_copy(cls_t[:], score_ps[:, 1, 0:EXPERTS]).then_inc(setup_act, 1)
            dve.wait_ge(setup_act, 2)
            dve.wait_ge(pool_consts, 4)

            def statistics(s, tile):
                for j in range(TILES):
                    last = dve.bn_stats(stats[:, j, :], tile(j))
                ordered(last)
                for j in range(TILES):
                    last = dve.bn_aggr(moments[:, j, :], stats[:, j, :])
                last.then_inc(moments_ready, 1)

            def normalise(s, k, dst, tile):
                dve.wait_ge(moments_ready, s * 4 + k)
                dve.wait_ge(rstd_ready, s * 4 + k)
                for j in range(TILES):
                    last = dve.tensor_scalar(dst[:, j, :], tile(j), moments[:, j, 0:1], rstd[:, j:j + 1],
                                             ALU.subtract, ALU.mult)
                return last

            def x_tile(s):
                return lambda j: x_all[:, bass.ds(s * TILES + j, 1), :].rearrange("p a h -> p (a h)")

            def first_norm(s):
                statistics(s, x_tile(s))
                normalise(s, 1, xn, x_tile(s)).then_inc(xn_ready, 1)

            def blocks_of(t, u):
                return t[:, u % 2, :].rearrange("p (g b k) -> p g b k", g=2, b=HALF)

            def shift_scores(s, u):
                n = s * len(STAGES) + u
                dve.wait_ge(scores_done, n + 1)
                found = score_ps[:].rearrange("p g (b k) -> p g b k", b=HALF)
                ordered(dve.tensor_reduce(row_max[:], found, AX_X, ALU.max))
                if u >= 2:
                    dve.wait_ge(probs_ready, n - 1)
                dve.tensor_tensor(blocks_of(shifted, u), found,
                                  row_max[:].unsqueeze(3).broadcast_to([P, 2, HALF, KW]),
                                  ALU.subtract).then_inc(shifted_ready, 1)

            def turn_probs(s, u):
                gp, hf = STAGES[u]
                dve.wait_ge(probs_ready, s * len(STAGES) + u + 1)
                dve.transpose(probs_t[:, 2 * gp:2 * gp + 2, hf * HALF * KW:(hf + 1) * HALF * KW],
                              probs[:, u % 2, :].rearrange("p (g c) -> p g c", g=2)).then_inc(probs_t_ready, 1)

            def divide_heads(s):
                dve.wait_ge(pv_done, s + 1)
                half = TILES // 2
                for i, ps in enumerate((work_a, work_b)):
                    last = dve.reciprocal(denom_inv[:, half * i:half * i + half],
                                          ps[:, 0:half * HG * GW].rearrange("p (j g c) -> p j g c", j=half, g=HG)[
                                              :, :, :, HPG * HD:])
                ordered(last)
                for i, ps in enumerate((work_a, work_b)):
                    last = dve.tensor_tensor(
                        heads_out[:, half * i:half * i + half, :].rearrange("p j (g h d) -> p (j g) h d", g=HG, h=HPG),
                        ps[:, 0:half * HG * GW].rearrange("p (j g c) -> p (j g) c", j=half, g=HG)[
                            :, :, 0:HPG * HD].rearrange("p a (h d) -> p a h d", h=HPG),
                        denom_inv[:, half * i:half * i + half].rearrange("p j g h -> p (j g) h").unsqueeze(
                            3).broadcast_to([P, half * HG, HPG, HD]),
                        ALU.mult)
                last.then_inc(heads_ready, 1)

            def attention_norm(s):
                dve.wait_ge(attn_done, s + 1)
                ordered(dve.tensor_tensor(attn[:], score_ps[:, 1, :].rearrange("p (j h) -> p j h", j=TILES),
                                             out_bias[:].unsqueeze(1).broadcast_to([P, TILES, P]), ALU.add))
                statistics(s, lambda j: attn[:, j, :])
                ordered(normalise(s, 2, attn_n, lambda j: attn[:, j, :]))
                ordered(dve.tensor_tensor(x1[:], x_all[:, bass.ds(s * TILES, TILES), :], attn_n[:], ALU.add))
                statistics(s, lambda j: x1[:, j, :])
                normalise(s, 3, x2, lambda j: x1[:, j, :]).then_inc(x2_ready, 1)

            def wide(t, n):
                return t[:].unsqueeze(2).broadcast_to([P, TILES, n])

            def route(s):
                dve.wait_ge(logits_done, s + 1)
                logits = work_b[:, 0:TILES * EXPERTS].rearrange("p (j e) -> p j e", j=TILES)
                ordered(dve.tensor_reduce(r_max[:], logits, AX_X, ALU.max))
                dve.tensor_tensor(r_shift[:], logits, wide(r_max, EXPERTS), ALU.subtract).then_inc(r_shift_ready, 1)
                dve.wait_ge(r_exp_ready, s + 1)
                ordered(dve.tensor_reduce(r_sum[:], r_exp[:], AX_X, ALU.add))
                ordered(dve.reciprocal(r_inv[:], r_sum[:]))
                ordered(dve.tensor_tensor(r_score[:], r_exp[:], wide(r_inv, EXPERTS), ALU.mult))
                dve.tensor_scalar(r_scaled[:], r_score[:], ROUTE_SCALE, None, ALU.mult)
                ordered(dve.tensor_tensor(r_biased[:, :, 0:EXPERTS], r_score[:],
                                             cls_bias_sb[:].unsqueeze(1).broadcast_to([P, TILES, EXPERTS]), ALU.add))
                for j in range(TILES):
                    last = dve.max(top8[:, j, :], r_biased[:, j, 0:EXPERTS])
                ordered(last)
                ordered(dve.memset(top8[:, :, TOPK:8], SENTINEL))
                for j in range(TILES):
                    last = dve.match_replace(r_marked[:, j, :], top8[:, j, :], r_biased[:, j, :], TAKEN)
                ordered(last)
                ordered(dve.scalar_tensor_tensor(out=r_weight[:], in0=r_marked[:, :, 0:EXPERTS], scalar=TAKEN,
                                                    in1=r_scaled[:], op0=ALU.is_equal, op1=ALU.mult))
                dve.tensor_reduce(zero_w[:], r_weight[:, :, ROUTED:EXPERTS], AX_X, ALU.add)
                ordered(dve.tensor_copy(route_hl[:, :, 0:ROUTED], r_weight[:, :, 0:ROUTED]))
                dve.tensor_tensor(route_hl[:, :, ROUTED:2 * ROUTED], r_weight[:, :, 0:ROUTED],
                                  route_hl[:, :, 0:ROUTED].bitcast(F32), ALU.subtract).then_inc(route_ready, 1)

            def gate_up(s, p):
                n = s * PAIRS + p
                dve.wait_ge(silu_ready, n + 1)
                dve.wait_ge(up_done, n + 1)
                dve.tensor_tensor(gated[:, p % 2, :], silu_sb[:, p % 2, :], up_ps[:], ALU.mult).then_inc(gated_ready, 1)
                dve.wait_ge(gated_ready, n + 1)
                dve.wait_ge(route_wide, n + 1)
                if p >= 2:
                    dve.wait_ge(h_lo_ready, n - 1)
                dve.tensor_tensor(hidden[:, p % 2, :], gated[:, p % 2, :], route_ps[:],
                                  ALU.mult).then_inc(hidden_ready, 1)

            def last_norm(s):
                dve.wait_ge(y_turned, s + 1)
                for j in range(TILES):
                    last = dve.scalar_tensor_tensor(out=ffn[:, j, :], in0=x2[:, j, :], scalar=zero_w[:, j:j + 1],
                                                    in1=work_b[:, P * j:P * (j + 1)], op0=ALU.mult, op1=ALU.add)
                ordered(last)
                statistics(s, lambda j: ffn[:, j, :])
                ordered(normalise(s, 4, ffn_n, lambda j: ffn[:, j, :]))
                dve.tensor_tensor(res_all[:, bass.ds(s * TILES, TILES), :], x1[:], ffn_n[:],
                                  ALU.add).then_inc(res_ready, 1)

            with dve.Fori(0, NSEQ) as s:
                steps[0] = 0
                dve.sem_clear(dve_step)
                first_norm(s)
                shift_scores(s, 0)
                for u in range(1, len(STAGES)):
                    shift_scores(s, u)
                    turn_probs(s, u - 1)
                turn_probs(s, len(STAGES) - 1)
                divide_heads(s)
                attention_norm(s)
                route(s)
                for p in range(PAIRS):
                    gate_up(s, p)
                last_norm(s)

        @block.tensor
        def _(pe):
            def turn_bank(n, tiles):
                if n >= 2:
                    pe.wait_ge(turned_hi, n - 1)
                    pe.wait_ge(turned_lo, n - 1)
                for i, t in enumerate(tiles):
                    last = pe.transpose((work_a, work_b)[n % 2][:, P * i:P * (i + 1)], t, ident)
                last.then_inc(turned, 1)

            pe.wait_ge(consts_in, 48)
            pe.wait_ge(gu_in, 64)
            for n in range(GU_BANKS):
                turn_bank(n, [gu_rows[:, 2 * n + i // 2, i % 2, :] for i in range(4)])
            pe.wait_ge(down_in, 16)
            for n in range(DOWN_BANKS):
                turn_bank(GU_BANKS + n, [down_rows[:, 4 * n + i, :] for i in range(4)])
            pe.wait_ge(tables_ready, 9)
            pe.wait_ge(small_in, 16 * SMALL)
            pe.matmul(score_ps[:, 0, 0:P], bv_wide[:], wo_sb[:], start=True, stop=True)
            pe.transpose(score_ps[:, 1, 0:EXPERTS], cls_sb[:], ident[0:EXPERTS, 0:EXPERTS]).then_inc(setup_pe, 1)
            pe.wait_ge(setup_act, 2)
            pe.wait_ge(pads_set, 4)

            def turn_tiles(ps, src):
                for j in range(TILES):
                    last = pe.transpose(ps[:, P * j:P * (j + 1)], src[:, j, :], ident)
                return last

            def turn_xn(s):
                pe.wait_ge(xn_ready, s + 1)
                turn_tiles(work_a, xn).then_inc(xn_turned, 1)

            def queries_keys(s):
                pe.wait_ge(xn_t_ready, s + 1)
                pe.matmul(work_b[:], wq_sb[:], xn_t[:, PAD:PAD + S], start=True, stop=True).then_inc(q_done, 1)
                pe.matmul(work_a[:], wk_sb[:], xn_t[:, PAD:PAD + S], start=True, stop=True).then_inc(k_done, 1)

            def values(s):
                for c in range(NC):
                    for h in range(HPG):
                        last = pe.matmul(score_ps[QB * h:QB * (h + 1), c * QB // 512, c * QB % 512:c * QB % 512 + QB],
                                         xn_t[:, QB * c:QB * (c + 1)],
                                         wv_sb[:].rearrange("i (g h d) -> i g h d", g=HG, h=HPG)[:, :, h, :],
                                         start=True, stop=True, skip_group_check=True)
                last.then_inc(v_done, 1)

            def scores(s, u):
                gp, hf = STAGES[u]
                n = s * len(STAGES) + u
                if u == 0:
                    pe.wait_ge(q_ready, 4 * (s + 1))
                    pe.wait_ge(k_ready, s + 1)
                    pe.wait_ge(v_ready, HPG * (s + 1))
                else:
                    pe.wait_ge(shifted_ready, n)
                for i in range(2):
                    pe.matmul(score_ps[:, i, :], ident_bf[:], band_bf[:, hf * 512:(hf + 1) * 512],
                              start=True, stop=False, skip_group_check=True)
                for b in range(HALF):
                    for i in range(2):
                        rows = slice(QB * (2 * gp + i), QB * (2 * gp + i + 1))
                        at = QB * (hf * HALF + b)
                        last = pe.matmul(score_ps[:, i, KW * b:KW * (b + 1)], q_blocks[rows, hf * HALF + b].rearrange("p h q -> p (h q)"),
                                         k_t[rows, at:at + KW], start=False, stop=True, skip_group_check=True)
                last.then_inc(scores_done, 1)

            def mix_values(s):
                pe.wait_ge(probs_t_ready, (s + 1) * len(STAGES))
                for j in range(TILES):
                    ps = (work_a, work_b)[j // (TILES // 2)]
                    for g in range(HG):
                        col = ((j % (TILES // 2)) * HG + g) * GW
                        for side in range(2):
                            for r in range(4):
                                b = 4 * j + r
                                at = b * KW + side * QB
                                last = pe.matmul(ps[QB * r:QB * (r + 1), col:col + GW], probs_t[:, g, at:at + QB],
                                                 v_blocks[:, b + side, g, :], start=(side == 0), stop=(side == 1),
                                                 skip_group_check=True)
                last.then_inc(pv_done, 1)

            def project_heads(s):
                pe.wait_ge(heads_ready, s + 1)
                turn_tiles(score_ps[:, 0, :], heads_out).then_inc(heads_turned, 1)
                pe.wait_ge(heads_t_ready, s + 1)
                for j in range(TILES):
                    last = pe.matmul(score_ps[:, 1, P * j:P * (j + 1)], heads_t[:, P * j:P * (j + 1)], wo_sb[:],
                                     start=True, stop=True)
                last.then_inc(attn_done, 1)

            def router(s):
                pe.wait_ge(x2_ready, s + 1)
                turn_tiles(work_a, x2).then_inc(x2_turned, 1)
                pe.wait_ge(x2_t_ready, s + 1)
                for j in range(TILES):
                    last = pe.matmul(work_b[:, EXPERTS * j:EXPERTS * (j + 1)], x2_t[:, P * j:P * (j + 1)], cls_t[:],
                                     start=True, stop=True)
                last.then_inc(logits_done, 1)
                pe.wait_ge(route_ready, s + 1)
                for j in range(TILES):
                    last = pe.transpose(work_a[:, P * j:P * (j + 1)], route_hl[:, j, :].bitcast(F32), ident)
                last.then_inc(route_turned, 1)

            def three_products(ps, w_hi, w_lo, a_hi, a_lo, start, stop):
                pe.matmul(ps, w_hi, a_hi, start=start, stop=False)
                pe.matmul(ps, w_hi, a_lo, start=False, stop=False)
                return pe.matmul(ps, w_lo, a_hi, start=False, stop=stop)

            def expert_up(s, p):
                n = s * PAIRS + p
                if p >= 1:
                    pe.wait_ge(silu_ready, n)
                three_products(gate_ps[:], gu_hi[:, p, 0, :], gu_lo[:, p, 0, :], x2_hi[:], x2_lo[:],
                               True, True).then_inc(gate_done, 1)
                if p >= 1:
                    pe.wait_ge(gated_ready, n)
                three_products(up_ps[:], gu_hi[:, p, 1, :], gu_lo[:, p, 1, :], x2_hi[:], x2_lo[:],
                               True, True).then_inc(up_done, 1)
                if p >= 1:
                    pe.wait_ge(hidden_ready, n)
                pe.matmul(route_ps[:], select[:, P * p:P * (p + 1)], route_t[:], start=True,
                          stop=True).then_inc(route_wide, 1)

            def expert_down(s, p):
                n = s * PAIRS + p
                pe.wait_ge(h_hi_ready, n + 1)
                pe.wait_ge(h_lo_ready, n + 1)
                three_products(y_ps[:], down_hi[:, p, :], down_lo[:, p, :], h_hi[:, p % 3, :], h_lo[:, p % 3, :],
                               p == 0, p == PAIRS - 1).then_inc(down_done, 1)

            def turn_y(s):
                pe.wait_ge(y_t_ready, s + 1)
                for j in range(TILES):
                    last = pe.transpose(work_b[:, P * j:P * (j + 1)], y_t[:, P * j:P * (j + 1)], ident)
                last.then_inc(y_turned, 1)

            with pe.Fori(0, NSEQ) as s:
                turn_xn(s)
                queries_keys(s)
                values(s)
                for u in range(len(STAGES)):
                    scores(s, u)
                mix_values(s)
                project_heads(s)
                router(s)
                pe.wait_ge(x2_hi_ready, s + 1)
                pe.wait_ge(x2_lo_ready, s + 1)
                pe.wait_ge(route_t_ready, s + 1)
                for p in range(PAIRS):
                    expert_up(s, p)
                    if p >= 2:
                        expert_down(s, p - 2)
                expert_down(s, PAIRS - 2)
                expert_down(s, PAIRS - 1)
                turn_y(s)


_INS = ["L0_attn_x", "L0_attn_Wq", "L0_attn_bq", "L0_attn_Wk", "L0_attn_bk", "L0_attn_Wv", "L0_attn_bv",
        "L0_attn_Wo", "L0_attn_bo", "L0_ffn_classifier_weight", "L0_ffn_e_score_correction_bias",
        "L0_ffn_gate_up_proj", "L0_ffn_down_proj"]


def kernel(**inputs):
    import concourse.bacc as bacc
    from concourse.bass_utils import run_bass_kernel_spmd

    nc = bacc.Bacc("TRN2", target_bir_lowering=False, num_devices=1)
    arrays = {f"in_{name}": np.ascontiguousarray(inputs[name]) for name in _INS}
    shape = inputs["L0_attn_x"].shape
    arrays["table"], arrays["band"], arrays["selector"] = shape_constants(shape[1])
    args = [nc.dram_tensor(name, a.shape, mybir.dt.from_np(a.dtype), kind="ExternalInput").ap()
            for name, a in arrays.items()]
    out = nc.dram_tensor("out", shape, F32, kind="ExternalOutput").ap()
    build_block(nc, *args, out)
    r = run_bass_kernel_spmd(nc, [arrays], core_ids=[0])
    return r.results[0]["out"]
```

```python
from contextlib import ExitStack

import numpy as np

import concourse.bass as bass
from concourse import mybir
from concourse.alu_op_type import AluOpType as ALU

ACT = mybir.ActivationFunctionType
F32 = mybir.dt.float32
F32R = mybir.dt.float32r
F16 = mybir.dt.float16
BF16 = mybir.dt.bfloat16
AX_X = mybir.AxisListType.X

P = 128
HEADS, HD = 16, 8
HG = 4
HPG = HEADS // HG
HALF_W = 16
QB = 32
KW = QB + 2 * HALF_W
NEG = -1e30
EPS = 1e-5
EXPERTS, ROUTED, TOPK = 40, 32, 6
PAIRS = ROUTED // 2
INNER = 64
ROUTE_SCALE = 2.5
TAKEN, SENTINEL = 3e38, -3e38


def shape_constants(S):
    nb = S // QB
    ident = np.eye(P, dtype=np.float32)
    p = np.arange(P)
    own_head = ((p[:, None] // HD) % HPG == np.arange(HPG)).astype(np.float32)
    table = np.concatenate([ident, own_head], axis=1)
    q = p % QB
    band = np.zeros((P, nb, KW), np.float32)
    for b in range(nb):
        query, key = b * QB + q[:, None], b * QB - HALF_W + np.arange(KW)[None, :]
        seen = (np.abs(query - key) <= HALF_W) & (key >= 0) & (key < S)
        band[:, b] = np.where(seen, 0.0, NEG)
    selector = np.zeros((P, PAIRS, P), np.float32)
    for pair in range(PAIRS):
        for m in range(P):
            e = 2 * pair + m // INNER
            selector[[e, ROUTED + e], pair, m] = 1.0
    return table, band.reshape(P, nb * KW), selector.reshape(P, PAIRS * P)


def build_block(nc, x, Wq, bq, Wk, bk, Wv, bv, Wo, bo, cls_w, cls_bias, w_gu, w_down, table, band, selector, out):
    NSEQ, S, _ = x.shape
    TILES = S // P
    NB = S // QB
    NC = NB + 1
    PAD = HALF_W
    SK = S + 2 * PAD
    HC = HD + 1
    GW = HPG * HC
    HALF = NB // 2
    HT = TILES // 2
    STAGES = [(hf, gp) for hf in range(2) for gp in range(HG // 2)]
    NSTAGE = len(STAGES)
    HB = 4
    LAG = 2
    GU_TURNS, DOWN_TURNS = PAIRS // 2, PAIRS // 4
    TURNS = GU_TURNS + DOWN_TURNS
    SMALL = 10
    POOL_SETS = 13
    TAIL = 2
    scale = 1.0 / float(np.sqrt(HD))

    with ExitStack() as ctx:
        def sb(name, shape, dt=F32):
            return ctx.enter_context(nc.sbuf_tensor(name, shape, dt))

        def sem(name):
            return ctx.enter_context(nc.semaphore(name))

        def bank(name):
            return ctx.enter_context(nc.psum_tensor(name, [P, 512], F32))

        gate_ps, up_ps, route_ps, y_ps = bank("gate_ps"), bank("up_ps"), bank("route_ps"), bank("y_ps")
        score_ps = ctx.enter_context(nc.psum_tensor("score_ps", [P, 2, 512], F32))
        work_a, work_b = bank("work_a"), bank("work_b")
        score_flat = score_ps[:].rearrange("p a c -> p (a c)")
        turn_ps = (gate_ps, up_ps, route_ps, y_ps)

        table_sb = sb("table_sb", [P, P + HPG])
        ident, own_head = table_sb[:, 0:P], table_sb[:, P:P + HPG]
        ident_bf = sb("ident_bf", [P, P], BF16)
        select = sb("select", [P, PAIRS * P], F32R)
        band_bf = sb("band_bf", [P, NB * KW], BF16)
        minus_half, minus_one, eps_sb = (sb(n, [P, TILES]) for n in ("minus_half", "minus_one", "eps_sb"))
        wq_sb, wk_sb, wv_sb, wo_sb = (sb(n, [P, P]) for n in ("wq_sb", "wk_sb", "wv_sb", "wo_sb"))
        bq_sb, bk_sb, bv_sb = (sb(n, [P, 1]) for n in ("bq_sb", "bk_sb", "bv_sb"))
        bv_wide, bo_wide, out_bias = (sb(n, [P, P]) for n in ("bv_wide", "bo_wide", "out_bias"))
        cls_sb, cls_t = sb("cls_sb", [EXPERTS, P]), sb("cls_t", [P, EXPERTS])
        cls_bias_sb = sb("cls_bias_sb", [P, EXPERTS])
        gu_hi, gu_lo = (sb(n, [P, PAIRS, 2, P], F32R) for n in ("gu_hi", "gu_lo"))
        down_hi, down_lo = (sb(n, [P, PAIRS, P], F32R) for n in ("down_hi", "down_lo"))

        x_sb, res = sb("x_sb", [P, TILES, P]), sb("res", [P, TILES, P])
        carry, kept = sb("carry", [P, 2, TILES, P]), sb("kept", [P, 2, TILES, P])
        x1, zero_part = carry[:, 0], carry[:, 1]
        stats, moments = sb("stats", [P, TILES, 6]), sb("moments", [P, TILES, 2])
        var_eps, neg_mean, rstd, shift = (sb(n, [P, TILES]) for n in ("var_eps", "neg_mean", "rstd", "shift"))
        y_stats, y_moments = sb("y_stats", [P, TILES, 6]), sb("y_moments", [P, TILES, 2])
        y_var_eps, y_neg_mean, y_rstd, y_shift = (
            sb(n, [P, TILES]) for n in ("y_var_eps", "y_neg_mean", "y_rstd", "y_shift"))
        xn, xn_t = sb("xn", [P, TILES, P]), sb("xn_t", [P, SK])
        q_f, k_f = sb("q_f", [P, S]), sb("k_f", [P, S])
        q_hi, q_lo = sb("q_hi", [P, S], F16), sb("q_lo", [P, S], F16)
        k_hi, k_lo = sb("k_hi", [P, SK], F16), sb("k_lo", [P, SK], F16)
        q_own_hi, q_own_lo = (sb(n, [P, NB, HPG, QB], F16) for n in ("q_own_hi", "q_own_lo"))
        v_rows = sb("v_rows", [P, TILES + 1, HEADS, HC])
        v_own = sb("v_own", [P, NC, HPG, HG * HC])
        row_max = sb("row_max", [P, 2, HALF])
        shifted, probs = sb("shifted", [P, 2, 2 * HALF * KW]), sb("probs", [P, 2, 2 * HALF * KW])
        probs_t = sb("probs_t", [P, 2, HG, HALF * KW])
        denom_inv = sb("denom_inv", [P, 2, HT * HEADS])
        heads_out, heads_t = sb("heads_out", [P, TILES, P]), sb("heads_t", [P, S])
        attn, attn_n = sb("attn", [P, TILES, P]), sb("attn_n", [P, TILES, P])
        x2, x2_t = sb("x2", [P, TILES, P]), sb("x2_t", [P, S])
        x2_hi, x2_lo = sb("x2_hi", [P, S], F32R), sb("x2_lo", [P, S], F32R)
        r_max, r_sum, r_inv, zero_w = (sb(n, [P, TILES]) for n in ("r_max", "r_sum", "r_inv", "zero_w"))
        r_shift, r_exp, r_score, r_scaled, r_weight = (
            sb(n, [P, TILES, EXPERTS]) for n in ("r_shift", "r_exp", "r_score", "r_scaled", "r_weight"))
        r_biased, r_marked = (sb(n, [P, TILES, EXPERTS + 2]) for n in ("r_biased", "r_marked"))
        top8 = sb("top8", [P, TILES, 8])
        route_hl = sb("route_hl", [P, TILES, P], F32R)
        route_t = sb("route_t", [P, S], F32R)
        pair_sb = sb("pair_sb", [P, 3, 2, S])
        silu_sb, gated, hidden = pair_sb[:, 0], pair_sb[:, 1], pair_sb[:, 2]
        h_hi, h_lo = sb("h_hi", [P, HB, S], F32R), sb("h_lo", [P, HB, S], F32R)
        y_t = sb("y_t", [P, S])
        tail_sb = sb("tail_sb", [P, 2, TILES, P])
        ffn, ffn_n = tail_sb[:, 0], tail_sb[:, 1]

        pair_flat = pair_sb[:].rearrange("p a b c -> p (a b c)")
        HP = PAIRS // 2
        gu_rows = [pair_flat[:, 0:PAIRS * P].rearrange("p (a s m) -> p a s m", s=2, m=P),
                   sb("gu_rows_1", [P, HP, 2, P])[:]]
        down_rows = [pair_flat[:, PAIRS * P:PAIRS * P + HP * P].rearrange("p (a m) -> p a m", m=P),
                     tail_sb[:].rearrange("p a j m -> p (a j) m")]

        x_in, table_in, small_in, gu_in, down_in, cast_in, out_done = map(sem, (
            "x_in", "table_in", "small_in", "gu_in", "down_in", "cast_in", "out_done"))
        kept_in = sem("kept_in")
        pool_consts = sem("pool_consts")
        dve_consts = sem("dve_consts")
        setup_pe, setup_done = sem("setup_pe"), sem("setup_done")
        turned, turned_hi, turned_lo = map(sem, ("turned", "turned_hi", "turned_lo"))
        dve_step, pool_step = sem("dve_step"), sem("pool_step")
        moments_ready, rstd_ready, xn_ready, attn_n_ready, x2_ready = map(sem, (
            "moments_ready", "rstd_ready", "xn_ready", "attn_n_ready", "x2_ready"))
        xn_turned, xn_t_ready, q_done, k_done, v_done = map(sem, (
            "xn_turned", "xn_t_ready", "q_done", "k_done", "v_done"))
        q_hi_ready, k_hi_ready, q_lo_ready, k_lo_ready, q_own_ready, v_rows_ready, v_own_in = map(sem, (
            "q_hi_ready", "k_hi_ready", "q_lo_ready", "k_lo_ready", "q_own_ready", "v_rows_ready", "v_own_in"))
        scores_done, shifted_ready, probs_ready, probs_t_ready = map(sem, (
            "scores_done", "shifted_ready", "probs_ready", "probs_t_ready"))
        pv_done, heads_ready, heads_turned, heads_t_ready, attn_done = map(sem, (
            "pv_done", "heads_ready", "heads_turned", "heads_t_ready", "attn_done"))
        x2_turned, x2_t_ready, x2_hi_ready, x2_lo_ready = map(sem, (
            "x2_turned", "x2_t_ready", "x2_hi_ready", "x2_lo_ready"))
        logits_done, r_shift_ready, r_exp_ready, zero_w_ready, route_ready, route_turned, route_t_ready = map(sem, (
            "logits_done", "r_shift_ready", "r_exp_ready", "zero_w_ready", "route_ready", "route_turned",
            "route_t_ready"))
        gate_done, up_done, route_wide, silu_ready, gated_ready, hidden_ready = map(sem, (
            "gate_done", "up_done", "route_wide", "silu_ready", "gated_ready", "hidden_ready"))
        h_hi_ready, h_lo_ready, down_done = map(sem, ("h_hi_ready", "h_lo_ready", "down_done"))
        y_t_ready, y_turned, zero_part_ready, y_moments_ready, y_rstd_ready, ffn_n_ready, res_ready = map(sem, (
            "y_t_ready", "y_turned", "zero_part_ready", "y_moments_ready", "y_rstd_ready", "ffn_n_ready", "res_ready"))

        def turn_target(n, gu, down):
            if n < GU_TURNS:
                return gu[:, 2 * n:2 * n + 2].rearrange("p a s m -> p (a s m)")
            n -= GU_TURNS
            return down[:, 4 * n:4 * n + 4].rearrange("p a m -> p (a m)")

        def at_least(eng, signal, count):
            if not (isinstance(count, int) and count <= 0):
                eng.wait_ge(signal, count)


        block = ctx.enter_context(nc.Block())

        @block.sync
        def _(sp):
            sp.dma_start(x_sb[:], x[0].rearrange("(j p) h -> p j h", p=P)).then_inc(x_in, 16)
            sp.dma_start(table_sb[:], table).then_inc(table_in, 16)
            for dst, src in ((wq_sb, Wq), (wk_sb, Wk), (wv_sb, Wv), (wo_sb, Wo)):
                sp.dma_start(dst[:], src).then_inc(small_in, 16)
            for dst, src in ((bq_sb, bq), (bk_sb, bk), (bv_sb, bv)):
                sp.dma_start(dst[:], src.rearrange("(p a) -> p a", a=1)).then_inc(small_in, 16)
            sp.dma_start(bo_wide[:], bo.partition_broadcast(P)).then_inc(small_in, 16)
            sp.dma_start(cls_bias_sb[:], cls_bias.partition_broadcast(P)).then_inc(small_in, 16)
            sp.dma_start(cls_sb[:], cls_w).then_inc(small_in, 16)
            gu = w_gu[0:ROUTED].rearrange("(p e) (s i) h -> e i p s h", e=2, s=2)
            down = w_down.rearrange("e h i -> h e i")
            for half in range(2):
                pairs = slice(HP * half, HP * (half + 1))
                for e in range(2):
                    for s in range(2):
                        sp.dma_start(gu_rows[half][INNER * e:INNER * (e + 1), :, s, :],
                                     gu[e, :, pairs, s, :]).then_inc(gu_in, 16)
                sp.dma_start(down_rows[half].rearrange("h p (e i) -> h (p e) i", e=2),
                             down[:, 2 * HP * half:2 * HP * (half + 1), :]).then_inc(down_in, 16)

            def spread_values(s):
                sp.wait_ge(v_rows_ready, 2 * (s + 1))
                for c in range(4):
                    rows, n = slice(QB * c, QB * (c + 1)), len(range(c, NC, 4))
                    for h in range(HPG):
                        sp.dma_start(v_own[QB * h:QB * (h + 1), c:NC:4, h, :],
                                     v_rows[rows, 0:n, HG * h:HG * (h + 1), :].rearrange("k n g d -> k n (g d)")
                                     ).then_inc(v_own_in, 16)

            def load(s):
                sp.wait_ge(moments_ready, 3 * s)
                sp.dma_start(x_sb[:], x[bass.ds(s, 1)].rearrange("a (j p) h -> p (a j) h", p=P)).then_inc(x_in, 16)

            def store(s):
                sp.wait_ge(res_ready, s + 1)
                sp.dma_start(out[bass.ds(s, 1)].rearrange("a (j p) h -> p (a j) h", p=P),
                             res[:]).then_inc(out_done, 16)

            def keep(s):
                sp.wait_ge(zero_part_ready, s + 1)
                sp.dma_start(kept[:], carry[:]).then_inc(kept_in, 16)

            spread_values(0)
            load(1)
            spread_values(1)
            keep(0)
            with sp.Fori(1, NSEQ - 1) as e:
                load(e + 1)
                spread_values(e + 1)
                store(e - 1)
                keep(e)
            store(NSEQ - 2)
            keep(NSEQ - 1)
            store(NSEQ - 1)
            sp.wait_ge(out_done, 16 * NSEQ)

        @block.gpsimd
        def _(pool):
            pool.dma_start(select[:], selector).then_inc(cast_in, 16)
            pool.dma_start(band_bf[:], band).then_inc(cast_in, 16)
            sets = [(minus_half[:], -0.5), (minus_one[:], -1.0), (eps_sb[:], EPS), (xn_t[:, 0:PAD], 0.0), (xn_t[:, PAD + S:], 0.0),
                    (k_hi[:, 0:PAD], 0.0), (k_hi[:, PAD + S:], 0.0), (k_lo[:, 0:PAD], 0.0), (k_lo[:, PAD + S:], 0.0),
                    (v_rows[:], 1.0), (v_own[:], 0.0), (r_biased[:], SENTINEL),
                    (route_hl[:, :, 2 * ROUTED:].bitcast(F32), 0.0)]
            assert len(sets) == POOL_SETS
            for dst, value in sets:
                pool.memset(dst, value).then_inc(pool_consts, 1)
            pool.wait_ge(pool_consts, POOL_SETS)
            steps = [0]

            def ordered(ins):
                steps[0] += 1
                ins.then_inc(pool_step, 1)
                pool.wait_ge(pool_step, steps[0])

            def inverse_deviation(m, v, neg, r, sh):
                ordered(pool.tensor_tensor(v[:], m[:, :, 1], eps_sb[:], ALU.add))
                pool.tensor_tensor(r[:], v[:], minus_half[:], ALU.pow)
                ordered(pool.tensor_tensor(neg[:], m[:, :, 0], minus_one[:], ALU.mult))
                return pool.tensor_tensor(sh[:], neg[:], r[:], ALU.mult)

            def deviations(s, k):
                pool.wait_ge(moments_ready, 3 * s + k)
                inverse_deviation(moments, var_eps, neg_mean, rstd, shift).then_inc(rstd_ready, 1)

            def low_queries_keys(s):
                pool.wait_ge(k_hi_ready, s + 1)
                pool.wait_ge(q_hi_ready, s + 1)
                pool.tensor_tensor(q_lo[:], q_f[:], q_hi[:], ALU.subtract).then_inc(q_lo_ready, 1)
                pool.tensor_tensor(k_lo[:, PAD:PAD + S], k_f[:], k_hi[:, PAD:PAD + S],
                                   ALU.subtract).then_inc(k_lo_ready, 1)

            def zero_experts(s):
                pool.wait_ge(zero_w_ready, s + 1)
                at_least(pool, kept_in, 16 * s)
                pool.tensor_tensor(zero_part, x2[:],
                                   zero_w[:].unsqueeze(2).broadcast_to([P, TILES, P]),
                                   ALU.mult).then_inc(zero_part_ready, 1)

            def hidden_low(e, p):
                n = e * PAIRS + p
                pool.wait_ge(h_hi_ready, n + 1)
                at_least(pool, down_done, n + 1 - HB)
                pool.tensor_tensor(h_lo[:, p % HB, :], hidden[:, p % 2, :], h_hi[:, p % HB, :].bitcast(F32),
                                   ALU.subtract).then_inc(h_lo_ready, 1)

            def tail_deviations(e):
                pool.wait_ge(y_moments_ready, e + 1)
                inverse_deviation(y_moments, y_var_eps, y_neg_mean, y_rstd, y_shift).then_inc(y_rstd_ready, 1)

            def tail_residual(e):
                pool.wait_ge(ffn_n_ready, TILES * (e + 1))
                at_least(pool, out_done, 16 * e)
                pool.tensor_tensor(res[:], kept[:, 0], ffn_n, ALU.add).then_inc(res_ready, 1)

            def step(e, a, tail):
                steps[0] = 0
                pool.sem_clear(pool_step)
                for p in range(PAIRS):
                    if e is not None and p >= 1:
                        hidden_low(e, p - 1)
                    if tail is not None and p == TAIL + 1:
                        tail_deviations(tail)
                    if tail is not None and p == TAIL + 2:
                        tail_residual(tail)
                    if a is None:
                        continue
                    if p == 0:
                        deviations(a, 1)
                    if p == 4:
                        low_queries_keys(a)
                    if p == 14:
                        deviations(a, 2)
                    if p == 15:
                        deviations(a, 3)
                if e is not None:
                    hidden_low(e, PAIRS - 1)
                if a is not None:
                    zero_experts(a)

            step(None, 0, None)
            step(0, 1, None)
            with pool.Fori(1, NSEQ - 1) as e:
                step(e, e + 1, e - 1)
            step(NSEQ - 1, None, NSEQ - 2)
            steps[0] = 0
            pool.sem_clear(pool_step)
            tail_deviations(NSEQ - 1)
            tail_residual(NSEQ - 1)

        @block.scalar
        def _(act):
            act.wait_ge(small_in, 16 * SMALL)
            act.wait_ge(pool_consts, POOL_SETS)

            def turned_high(n):
                if n < TURNS:
                    act.wait_ge(turned, n + 1)
                    act.activation(turn_target(n, gu_hi, down_hi), turn_ps[n % 4][:], ACT.Copy).then_inc(turned_hi, 1)

            def normalise(dst, src, r, sh, signal):
                for j in range(TILES):
                    act.activation(dst[:, j, :], src(j), ACT.Identity, bias=sh[:, j:j + 1],
                                   scale=r[:, j:j + 1]).then_inc(signal, 1)

            def first_norm(s):
                act.wait_ge(rstd_ready, 3 * s + 1)
                normalise(xn, lambda j: x_sb[:, j, :], rstd, shift, xn_ready)

            def turn_xn(s):
                act.wait_ge(xn_turned, s + 1)
                act.activation(xn_t[:, PAD:PAD + S], work_a[:], ACT.Copy).then_inc(xn_t_ready, 1)

            def queries_keys(s):
                act.wait_ge(q_done, s + 1)
                act.activation(q_hi[:], work_b[:], ACT.Identity, bias=bq_sb[:, 0:1])
                act.activation(q_f[:], work_b[:], ACT.Identity, bias=bq_sb[:, 0:1]).then_inc(q_hi_ready, 1)
                act.wait_ge(k_done, s + 1)
                act.activation(k_hi[:, PAD:PAD + S], work_a[:], ACT.Identity, bias=bk_sb[:, 0:1])
                act.activation(k_f[:], work_a[:], ACT.Identity, bias=bk_sb[:, 0:1]).then_inc(k_hi_ready, 1)

            def values(s):
                act.wait_ge(v_done, s + 1)
                act.activation(v_rows[:, 0:TILES, :, 0:HD],
                               score_ps[:, 0, :].rearrange("p (j h d) -> p j h d", h=HEADS, d=HD),
                               ACT.Copy).then_inc(v_rows_ready, 1)
                act.activation(v_rows[0:QB, TILES, :, 0:HD],
                               score_ps[0:QB, 1, 0:P].rearrange("p (h d) -> p h d", d=HD),
                               ACT.Copy).then_inc(v_rows_ready, 1)

            def exponentials(s, u):
                n = s * NSTAGE + u
                act.wait_ge(shifted_ready, n + 1)
                at_least(act, probs_t_ready, n - 1)
                act.activation(probs[:, u % 2, :], shifted[:, u % 2, :], ACT.Exp, scale=scale).then_inc(probs_ready, 1)

            def turn_heads(s):
                act.wait_ge(heads_turned, s + 1)
                act.activation(heads_t[:], score_ps[:, 0, :], ACT.Copy).then_inc(heads_t_ready, 1)

            def attention_norm(s):
                act.wait_ge(rstd_ready, 3 * s + 2)
                normalise(attn_n, lambda j: attn[:, j, :], rstd, shift, attn_n_ready)

            def second_norm(s):
                act.wait_ge(rstd_ready, 3 * s + 3)
                normalise(x2, lambda j: x1[:, j, :], rstd, shift, x2_ready)

            def turn_x2(s):
                act.wait_ge(x2_turned, s + 1)
                act.activation(x2_t[:], work_a[:], ACT.Copy).then_inc(x2_t_ready, 1)

            def route_exp(s):
                act.wait_ge(r_shift_ready, s + 1)
                act.activation(r_exp[:], r_shift[:], ACT.Exp).then_inc(r_exp_ready, 1)

            def high_x2(s):
                at_least(act, up_done, s * PAIRS)
                act.activation(x2_hi[:], work_a[:], ACT.Copy).then_inc(x2_hi_ready, 1)

            def turn_route(s):
                act.wait_ge(route_turned, s + 1)
                at_least(act, route_wide, s * PAIRS)
                act.activation(route_t[:], score_ps[:, 0, :], ACT.Copy).then_inc(route_t_ready, 1)

            def silu(e, p):
                n = e * PAIRS + p
                act.wait_ge(gate_done, n + 1)
                at_least(act, gated_ready, n - 1)
                act.activation(silu_sb[:, p % 2, :], gate_ps[:], ACT.Silu).then_inc(silu_ready, 1)

            def hidden_high(e, p):
                n = e * PAIRS + p
                act.wait_ge(hidden_ready, n + 1)
                at_least(act, down_done, n + 1 - HB)
                act.activation(h_hi[:, p % HB, :], hidden[:, p % 2, :], ACT.Copy).then_inc(h_hi_ready, 1)

            def take_y(e):
                act.wait_ge(down_done, (e + 1) * PAIRS)
                act.activation(y_t[:], y_ps[:], ACT.Copy).then_inc(y_t_ready, 1)

            def tail_norm(e):
                act.wait_ge(y_rstd_ready, e + 1)
                normalise(ffn_n, lambda j: ffn[:, j, :], y_rstd, y_shift, ffn_n_ready)

            def step(e, a, tail):
                for p in range(PAIRS):
                    if e is not None:
                        silu(e, p)
                        if p >= 1:
                            hidden_high(e, p - 1)
                    else:
                        turned_high(p)
                    if tail is not None and p == TAIL - 1:
                        take_y(tail)
                    if tail is not None and p == TAIL + 2:
                        tail_norm(tail)
                    if a is None:
                        continue
                    if p == 1:
                        first_norm(a)
                    if p == 2:
                        turn_xn(a)
                    if p == 3:
                        queries_keys(a)
                    if p == 4:
                        values(a)
                    if p == 7:
                        exponentials(a, 0)
                        exponentials(a, 1)
                    if p == 10:
                        exponentials(a, 2)
                        exponentials(a, 3)
                    if p == 12:
                        turn_heads(a)
                    if p == 14:
                        attention_norm(a)
                    if p == 15:
                        second_norm(a)
                if e is not None:
                    hidden_high(e, PAIRS - 1)
                if a is not None:
                    turn_x2(a)
                    high_x2(a)
                    route_exp(a)
                    turn_route(a)

            step(None, 0, None)
            step(0, 1, None)
            with act.Fori(1, NSEQ - 1) as e:
                step(e, e + 1, e - 1)
            step(NSEQ - 1, None, NSEQ - 2)
            take_y(NSEQ - 1)
            tail_norm(NSEQ - 1)

        @block.vector
        def _(dve):
            steps = [0]

            def ordered(ins):
                steps[0] += 1
                ins.then_inc(dve_step, 1)
                dve.wait_ge(dve_step, steps[0])

            def turned_low(n):
                if n < TURNS:
                    dve.wait_ge(turned_hi, n + 1)
                    dve.tensor_tensor(turn_target(n, gu_lo, down_lo), turn_ps[n % 4][:],
                                      turn_target(n, gu_hi, down_hi).bitcast(F32),
                                      ALU.subtract).then_inc(turned_lo, 1)

            def statistics(st, m, tile):
                for j in range(TILES):
                    last = dve.bn_stats(st[:, j, :], tile(j))
                ordered(last)
                for j in range(TILES):
                    last = dve.bn_aggr(m[:, j, :], st[:, j, :])
                return last

            def first_statistics(s):
                dve.wait_ge(x_in, 16 * (s + 1))
                statistics(stats, moments, lambda j: x_sb[:, j, :]).then_inc(moments_ready, 1)

            def own_queries(s):
                dve.wait_ge(q_hi_ready, s + 1)
                dve.wait_ge(q_lo_ready, s + 1)
                for dst, src in ((q_own_hi, q_hi), (q_own_lo, q_lo)):
                    for h in range(HPG):
                        dve.tensor_scalar(dst[:, :, h, :], src[:].rearrange("p (b q) -> p b q", b=NB),
                                          own_head[:, h:h + 1], None, ALU.mult).then_inc(q_own_ready, 1)

            def blocks_of(t, u):
                return t[:, u % 2, :].rearrange("p (g b k) -> p g b k", g=2, b=HALF)

            def shift_scores(s, u):
                n = s * NSTAGE + u
                dve.wait_ge(scores_done, n + 1)
                found = score_ps[:].rearrange("p g (b k) -> p g b k", b=HALF)
                ordered(dve.tensor_reduce(row_max[:], found, AX_X, ALU.max))
                at_least(dve, probs_ready, n - 1)
                dve.tensor_tensor(blocks_of(shifted, u), found,
                                  row_max[:].unsqueeze(3).broadcast_to([P, 2, HALF, KW]),
                                  ALU.subtract).then_inc(shifted_ready, 1)

            def turn_probs(s, u):
                hf, gp = STAGES[u]
                dve.wait_ge(probs_ready, s * NSTAGE + u + 1)
                dve.transpose(probs_t[:, hf, 2 * gp:2 * gp + 2, :],
                              probs[:, u % 2, :].rearrange("p (g c) -> p g c", g=2)).then_inc(probs_t_ready, 1)

            def divide_heads(s, hf):
                dve.wait_ge(pv_done, 2 * s + hf + 1)
                sums = (work_a, work_b)[hf][:, 0:HT * HEADS * HC].rearrange("p (a c) -> p a c", c=HC)
                ordered(dve.reciprocal(denom_inv[:, hf, :], sums[:, :, HD]))
                dve.tensor_tensor(heads_out[:, HT * hf:HT * (hf + 1), :].rearrange("p j (a d) -> p (j a) d", d=HD),
                                  sums[:, :, 0:HD], denom_inv[:, hf, :].unsqueeze(2).broadcast_to([P, HT * HEADS, HD]),
                                  ALU.mult).then_inc(heads_ready, 1)

            def attention_statistics(s):
                dve.wait_ge(attn_done, s + 1)
                ordered(dve.tensor_tensor(attn[:], score_ps[:, 1, :].rearrange("p (j h) -> p j h", j=TILES),
                                          out_bias[:].unsqueeze(1).broadcast_to([P, TILES, P]), ALU.add))
                statistics(stats, moments, lambda j: attn[:, j, :]).then_inc(moments_ready, 1)

            def second_statistics(s):
                dve.wait_ge(attn_n_ready, TILES * (s + 1))
                at_least(dve, kept_in, 16 * s)
                ordered(dve.tensor_tensor(x1, x_sb[:], attn_n[:], ALU.add))
                statistics(stats, moments, lambda j: x1[:, j, :]).then_inc(moments_ready, 1)

            def wide(t):
                return t[:].unsqueeze(2).broadcast_to([P, TILES, EXPERTS])

            def route(s):
                dve.wait_ge(logits_done, s + 1)
                logits = work_b[:, 0:TILES * EXPERTS].rearrange("p (j e) -> p j e", j=TILES)
                ordered(dve.tensor_reduce(r_max[:], logits, AX_X, ALU.max))
                dve.tensor_tensor(r_shift[:], logits, wide(r_max), ALU.subtract).then_inc(r_shift_ready, 1)
                dve.wait_ge(r_exp_ready, s + 1)
                ordered(dve.tensor_reduce(r_sum[:], r_exp[:], AX_X, ALU.add))
                ordered(dve.reciprocal(r_inv[:], r_sum[:]))
                ordered(dve.tensor_tensor(r_score[:], r_exp[:], wide(r_inv), ALU.mult))
                dve.tensor_scalar(r_scaled[:], r_score[:], ROUTE_SCALE, None, ALU.mult)
                ordered(dve.tensor_tensor(r_biased[:, :, 0:EXPERTS], r_score[:],
                                          cls_bias_sb[:].unsqueeze(1).broadcast_to([P, TILES, EXPERTS]), ALU.add))
                for j in range(TILES):
                    last = dve.max(top8[:, j, :], r_biased[:, j, 0:EXPERTS])
                ordered(last)
                ordered(dve.memset(top8[:, :, TOPK:8], SENTINEL))
                for j in range(TILES):
                    last = dve.match_replace(r_marked[:, j, :], top8[:, j, :], r_biased[:, j, :], TAKEN)
                ordered(last)
                ordered(dve.scalar_tensor_tensor(out=r_weight[:], in0=r_marked[:, :, 0:EXPERTS], scalar=TAKEN,
                                                 in1=r_scaled[:], op0=ALU.is_equal, op1=ALU.mult))
                dve.tensor_reduce(zero_w[:], r_weight[:, :, ROUTED:EXPERTS], AX_X, ALU.add).then_inc(zero_w_ready, 1)
                ordered(dve.tensor_copy(route_hl[:, :, 0:ROUTED], r_weight[:, :, 0:ROUTED]))
                dve.tensor_tensor(route_hl[:, :, ROUTED:2 * ROUTED], r_weight[:, :, 0:ROUTED],
                                  route_hl[:, :, 0:ROUTED].bitcast(F32), ALU.subtract).then_inc(route_ready, 1)

            def low_x2(s):
                dve.wait_ge(x2_hi_ready, s + 1)
                dve.tensor_tensor(x2_lo[:], x2_t[:], x2_hi[:].bitcast(F32), ALU.subtract).then_inc(x2_lo_ready, 1)

            def gate_up(e, p):
                n = e * PAIRS + p
                dve.wait_ge(silu_ready, n + 1)
                dve.wait_ge(up_done, n + 1)
                dve.tensor_tensor(gated[:, p % 2, :], silu_sb[:, p % 2, :], up_ps[:], ALU.mult).then_inc(gated_ready, 1)
                dve.wait_ge(gated_ready, n + 1)
                dve.wait_ge(route_wide, n + 1)
                at_least(dve, h_lo_ready, n - 1)
                dve.tensor_tensor(hidden[:, p % 2, :], gated[:, p % 2, :], route_ps[:],
                                  ALU.mult).then_inc(hidden_ready, 1)

            def tail_statistics(e):
                dve.wait_ge(y_turned, e + 1)
                dve.wait_ge(kept_in, 16 * (e + 1))
                ordered(dve.tensor_tensor(ffn, work_b[:].rearrange("p (j h) -> p j h", j=TILES),
                                          kept[:, 1], ALU.add))
                statistics(y_stats, y_moments, lambda j: ffn[:, j, :]).then_inc(y_moments_ready, 1)

            def step(e, a, tail):
                steps[0] = 0
                dve.sem_clear(dve_step)
                for p in range(PAIRS):
                    if e is not None:
                        gate_up(e, p)
                    else:
                        turned_low(p)
                    if tail is not None and p == TAIL:
                        tail_statistics(tail)
                    if a is None:
                        continue
                    if p == 0:
                        first_statistics(a)
                    if p == 4:
                        own_queries(a)
                    if p == 5:
                        shift_scores(a, 0)
                    if p == 6:
                        shift_scores(a, 1)
                    if p == 7:
                        turn_probs(a, 0)
                        turn_probs(a, 1)
                    if p == 8:
                        shift_scores(a, 2)
                    if p == 9:
                        shift_scores(a, 3)
                    if p == 10:
                        divide_heads(a, 0)
                        turn_probs(a, 2)
                        turn_probs(a, 3)
                    if p == 11:
                        divide_heads(a, 1)
                    if p == 13:
                        attention_statistics(a)
                    if p == 14:
                        second_statistics(a)
                if a is not None:
                    low_x2(a)
                    route(a)

            dve.wait_ge(table_in, 16)
            dve.tensor_copy(ident_bf[:], ident).then_inc(dve_consts, 1)
            dve.wait_ge(small_in, 16 * SMALL)
            dve.tensor_copy(bv_wide[:], bv_sb[:, 0:1].broadcast_to([P, P])).then_inc(dve_consts, 1)
            dve.wait_ge(pool_consts, POOL_SETS)
            dve.wait_ge(setup_pe, 1)
            dve.tensor_tensor(out_bias[:], score_ps[:, 0, 0:P], bo_wide[:], ALU.add).then_inc(setup_done, 1)
            dve.tensor_copy(cls_t[:], score_ps[:, 1, 0:EXPERTS]).then_inc(setup_done, 1)
            dve.wait_ge(setup_done, 2)
            step(None, 0, None)
            step(0, 1, None)
            with dve.Fori(1, NSEQ - 1) as e:
                step(e, e + 1, e - 1)
            step(NSEQ - 1, None, NSEQ - 2)
            steps[0] = 0
            dve.sem_clear(dve_step)
            tail_statistics(NSEQ - 1)

        @block.tensor
        def _(pe):
            def turn_weights(n):
                if n >= TURNS:
                    return
                at_least(pe, turned_hi, n - 3)
                at_least(pe, turned_lo, n - 3)
                if n < GU_TURNS:
                    if n % (GU_TURNS // 2) == 0:
                        pe.wait_ge(gu_in, 128)
                    half, first = divmod(2 * n, HP)
                    tiles = [gu_rows[half][:, first + i // 2, i % 2, :] for i in range(4)]
                else:
                    pe.wait_ge(down_in, 32)
                    half, first = divmod(4 * (n - GU_TURNS), HP)
                    tiles = [down_rows[half][:, first + i, :] for i in range(4)]
                for i, t in enumerate(tiles):
                    last = pe.transpose(turn_ps[n % 4][:, P * i:P * (i + 1)], t, ident)
                last.then_inc(turned, 1)

            def turn_tiles(ps, src):
                for j in range(TILES):
                    last = pe.transpose(ps[:, P * j:P * (j + 1)], src[:, j, :], ident)
                return last

            def turn_xn(s):
                pe.wait_ge(xn_ready, TILES * (s + 1))
                turn_tiles(work_a, xn).then_inc(xn_turned, 1)

            def queries_keys(s):
                pe.wait_ge(xn_t_ready, s + 1)
                at_least(pe, y_moments_ready, s - 1)
                pe.matmul(work_b[:], wq_sb[:], xn_t[:, PAD:PAD + S], start=True, stop=True).then_inc(q_done, 1)
                pe.matmul(work_a[:], wk_sb[:], xn_t[:, PAD:PAD + S], start=True, stop=True).then_inc(k_done, 1)

            def values(s):
                at_least(pe, route_t_ready, s)
                for j in range(TILES + 1):
                    keys = min(P, SK - P * j)
                    last = pe.matmul(score_flat[0:keys, P * j:P * (j + 1)], xn_t[:, P * j:P * j + keys],
                                     wv_sb[:].rearrange("i (g h d) -> i h g d", g=HG, h=HPG), start=True, stop=True)
                last.then_inc(v_done, 1)

            def scores(s, u):
                hf, gp = STAGES[u]
                n = s * NSTAGE + u
                if u == 0:
                    pe.wait_ge(q_own_ready, 2 * HPG * (s + 1))
                    pe.wait_ge(k_lo_ready, s + 1)
                    pe.wait_ge(v_rows_ready, 2 * (s + 1))
                else:
                    pe.wait_ge(shifted_ready, n)
                for i in range(2):
                    pe.matmul(score_ps[:, i, :], ident_bf[:], band_bf[:, hf * 512:(hf + 1) * 512],
                              start=True, stop=False, skip_group_check=True)
                for b in range(HALF):
                    at = QB * (hf * HALF + b)
                    for q, k in ((q_own_hi, k_hi), (q_own_hi, k_lo), (q_own_lo, k_hi)):
                        for i in range(2):
                            rows = slice(QB * (2 * gp + i), QB * (2 * gp + i + 1))
                            last = pe.matmul(score_ps[:, i, KW * b:KW * (b + 1)],
                                             q[rows, hf * HALF + b].rearrange("p h q -> p (h q)"),
                                             k[rows, at:at + KW], start=False, stop=(k is k_hi and q is q_own_lo),
                                             skip_group_check=True)
                last.then_inc(scores_done, 1)

            def mix_values(s, hf, j):
                if j == 0:
                    pe.wait_ge(probs_t_ready, s * NSTAGE + 2 * (hf + 1))
                    pe.wait_ge(v_own_in, 16 * 4 * HPG * (s + 1))
                for g in range(HG):
                    col = (j * HG + g) * GW
                    for side in range(2):
                        for r in range(4):
                            b = 4 * j + r
                            last = pe.matmul((work_a, work_b)[hf][QB * r:QB * (r + 1), col:col + GW],
                                             probs_t[:, hf, g, b * KW + side * QB:b * KW + (side + 1) * QB],
                                             v_own[:, hf * HALF + b + side, :, HC * g:HC * (g + 1)],
                                             start=(side == 0), stop=(side == 1), skip_group_check=True)
                if j == HT - 1:
                    last.then_inc(pv_done, 1)

            def turn_heads(s):
                pe.wait_ge(heads_ready, 2 * (s + 1))
                pe.wait_ge(shifted_ready, NSTAGE * (s + 1))
                turn_tiles(score_ps[:, 0, :], heads_out).then_inc(heads_turned, 1)

            def project_heads(s):
                pe.wait_ge(heads_t_ready, s + 1)
                for j in range(TILES):
                    last = pe.matmul(score_ps[:, 1, P * j:P * (j + 1)], heads_t[:, P * j:P * (j + 1)], wo_sb[:],
                                     start=True, stop=True)
                last.then_inc(attn_done, 1)

            def turn_x2(s):
                pe.wait_ge(x2_ready, TILES * (s + 1))
                turn_tiles(work_a, x2).then_inc(x2_turned, 1)

            def logits(s):
                pe.wait_ge(x2_t_ready, s + 1)
                for j in range(TILES):
                    last = pe.matmul(work_b[:, EXPERTS * j:EXPERTS * (j + 1)], x2_t[:, P * j:P * (j + 1)], cls_t[:],
                                     start=True, stop=True)
                last.then_inc(logits_done, 1)

            def turn_route(s):
                pe.wait_ge(route_ready, s + 1)
                for j in range(TILES):
                    last = pe.transpose(score_ps[:, 0, P * j:P * (j + 1)], route_hl[:, j, :].bitcast(F32), ident)
                last.then_inc(route_turned, 1)

            def three_products(ps, w_hi, w_lo, a_hi, a_lo, start, stop):
                pe.matmul(ps, w_hi, a_hi, start=start, stop=False)
                pe.matmul(ps, w_lo, a_hi, start=False, stop=False)
                return pe.matmul(ps, w_hi, a_lo, start=False, stop=stop)

            def expert_up(e, p):
                n = e * PAIRS + p
                if p == 0:
                    pe.wait_ge(x2_hi_ready, e + 1)
                    pe.wait_ge(x2_lo_ready, e + 1)
                at_least(pe, silu_ready, n)
                three_products(gate_ps[:], gu_hi[:, p, 0, :], gu_lo[:, p, 0, :], x2_hi[:], x2_lo[:],
                               True, True).then_inc(gate_done, 1)
                at_least(pe, gated_ready, n)
                three_products(up_ps[:], gu_hi[:, p, 1, :], gu_lo[:, p, 1, :], x2_hi[:], x2_lo[:],
                               True, True).then_inc(up_done, 1)
                if p == 0:
                    pe.wait_ge(route_t_ready, e + 1)
                at_least(pe, hidden_ready, n)
                pe.matmul(route_ps[:], select[:, P * p:P * (p + 1)], route_t[:], start=True,
                          stop=True).then_inc(route_wide, 1)

            def expert_down(e, p):
                n = e * PAIRS + p
                pe.wait_ge(h_hi_ready, n + 1)
                pe.wait_ge(h_lo_ready, n + 1)
                if p == 0:
                    at_least(pe, y_t_ready, e)
                three_products(y_ps[:], down_hi[:, p, :], down_lo[:, p, :], h_hi[:, p % HB, :], h_lo[:, p % HB, :],
                               p == 0, p == PAIRS - 1).then_inc(down_done, 1)

            def turn_y(e):
                pe.wait_ge(y_t_ready, e + 1)
                for j in range(TILES):
                    last = pe.transpose(work_b[:, P * j:P * (j + 1)], y_t[:, P * j:P * (j + 1)], ident)
                last.then_inc(y_turned, 1)

            def step(e, a, tail):
                for p in range(PAIRS):
                    if e is not None:
                        expert_up(e, p)
                        if p >= LAG:
                            expert_down(e, p - LAG)
                        elif tail is not None:
                            expert_down(tail, PAIRS - LAG + p)
                    else:
                        turn_weights(p)
                    if tail is not None and p == TAIL:
                        turn_y(tail)
                    if a is None:
                        continue
                    if p == 2:
                        turn_xn(a)
                    if p == 3:
                        queries_keys(a)
                        values(a)
                    if p == 5:
                        scores(a, 0)
                    if p == 6:
                        scores(a, 1)
                    if p == 8:
                        scores(a, 2)
                        mix_values(a, 0, 0)
                    if p == 9:
                        scores(a, 3)
                        mix_values(a, 0, 1)
                    if p == 11:
                        mix_values(a, 1, 0)
                        mix_values(a, 1, 1)
                    if p == 12:
                        turn_heads(a)
                    if p == 13:
                        project_heads(a)
                if a is not None:
                    turn_x2(a)
                    logits(a)
                    turn_route(a)

            pe.wait_ge(table_in, 16)
            pe.wait_ge(small_in, 16 * SMALL)
            pe.wait_ge(cast_in, 32)
            pe.wait_ge(pool_consts, POOL_SETS)
            pe.wait_ge(dve_consts, 2)
            pe.matmul(score_ps[:, 0, 0:P], bv_wide[:], wo_sb[:], start=True, stop=True)
            pe.transpose(score_ps[:, 1, 0:EXPERTS], cls_sb[:], ident[0:EXPERTS, 0:EXPERTS]).then_inc(setup_pe, 1)
            pe.wait_ge(setup_done, 2)
            step(None, 0, None)
            step(0, 1, None)
            with pe.Fori(1, NSEQ - 1) as e:
                step(e, e + 1, e - 1)
            step(NSEQ - 1, None, NSEQ - 2)
            expert_down(NSEQ - 1, PAIRS - 2)
            expert_down(NSEQ - 1, PAIRS - 1)
            turn_y(NSEQ - 1)


_INS = ["L0_attn_x", "L0_attn_Wq", "L0_attn_bq", "L0_attn_Wk", "L0_attn_bk", "L0_attn_Wv", "L0_attn_bv",
        "L0_attn_Wo", "L0_attn_bo", "L0_ffn_classifier_weight", "L0_ffn_e_score_correction_bias",
        "L0_ffn_gate_up_proj", "L0_ffn_down_proj"]


def kernel(**inputs):
    import concourse.bacc as bacc
    from concourse.bass_utils import run_bass_kernel_spmd

    nc = bacc.Bacc("TRN2", target_bir_lowering=False, num_devices=1)
    arrays = {f"in_{name}": np.ascontiguousarray(inputs[name]) for name in _INS}
    shape = inputs["L0_attn_x"].shape
    arrays["table"], arrays["band"], arrays["selector"] = shape_constants(shape[1])
    args = [nc.dram_tensor(name, a.shape, mybir.dt.from_np(a.dtype), kind="ExternalInput").ap()
            for name, a in arrays.items()]
    out = nc.dram_tensor("out", shape, F32, kind="ExternalOutput").ap()
    build_block(nc, *args, out)
    r = run_bass_kernel_spmd(nc, [arrays], core_ids=[0])
    return r.results[0]["out"]
```

```python
from contextlib import ExitStack

import numpy as np

import concourse.bass as bass
from concourse import mybir
from concourse.alu_op_type import AluOpType as ALU

ACT = mybir.ActivationFunctionType
F32 = mybir.dt.float32
F32R = mybir.dt.float32r
F16 = mybir.dt.float16
BF16 = mybir.dt.bfloat16
AX_X = mybir.AxisListType.X

P = 128
HEADS, HD = 16, 8
HG = 4
HPG = HEADS // HG
HALF_W = 16
QB = 32
KW = QB + 2 * HALF_W
NEG = -1e30
EPS = 1e-5
EXPERTS, ROUTED, TOPK = 40, 32, 6
PAIRS = ROUTED // 2
INNER = 64
ROUTE_SCALE = 2.5
TAKEN, SENTINEL = 3e38, -3e38


def shape_constants(S):
    nb = S // QB
    ident = np.eye(P, dtype=np.float32)
    p = np.arange(P)
    own_head = ((p[:, None] // HD) % HPG == np.arange(HPG)).astype(np.float32)
    table = np.concatenate([ident, own_head], axis=1)
    q = p % QB
    band = np.zeros((P, nb, KW), np.float32)
    for b in range(nb):
        query, key = b * QB + q[:, None], b * QB - HALF_W + np.arange(KW)[None, :]
        seen = (np.abs(query - key) <= HALF_W) & (key >= 0) & (key < S)
        band[:, b] = np.where(seen, 0.0, NEG)
    selector = np.zeros((P, PAIRS, P), np.float32)
    for pair in range(PAIRS):
        for m in range(P):
            e = 2 * pair + m // INNER
            selector[[e, ROUTED + e], pair, m] = 1.0
    return table, band.reshape(P, nb * KW), selector.reshape(P, PAIRS * P)


def build_block(nc, x, Wq, bq, Wk, bk, Wv, bv, Wo, bo, cls_w, cls_bias, w_gu, w_down, table, band, selector, out):
    NSEQ, S, _ = x.shape
    TILES = S // P
    NB = S // QB
    NC = NB + 1
    PAD = HALF_W
    SK = S + 2 * PAD
    HC = HD + 1
    GW = HPG * HC
    PARTS = 3
    HALF = NB // 2
    HT = TILES // 2
    STAGES = [(hf, gp) for gp in range(HG // 2) for hf in range(2)]
    NSTAGE = len(STAGES)
    HB = 4
    LAG = 3
    EARLY, LATE = range(PAIRS // 2), range(-PAIRS // 2, 0)
    GU_TURNS, DOWN_TURNS = PAIRS // 2, PAIRS // 4
    TURNS = GU_TURNS + DOWN_TURNS
    FRONT, BACK = 5, 5
    POOL_SETS, DVE_SETS = 10, 3
    scale = 1.0 / float(np.sqrt(HD))

    with ExitStack() as ctx:
        def sb(name, shape, dt=F32):
            return ctx.enter_context(nc.sbuf_tensor(name, shape, dt))

        def sem(name):
            return ctx.enter_context(nc.semaphore(name))

        def bank(name):
            return ctx.enter_context(nc.psum_tensor(name, [P, 512], F32))

        gate_ps, up_ps, route_ps, y_ps = bank("gate_ps"), bank("up_ps"), bank("route_ps"), bank("y_ps")
        score_ps = ctx.enter_context(nc.psum_tensor("score_ps", [P, 2, 512], F32))
        work_a, work_b = bank("work_a"), bank("work_b")
        score_flat = score_ps[:].rearrange("p a c -> p (a c)")
        turn_ps = (gate_ps, up_ps, route_ps, y_ps)

        table_sb = sb("table_sb", [P, P + HPG])
        ident, own_head = table_sb[:, 0:P], table_sb[:, P:P + HPG]
        ident_bf = sb("ident_bf", [P, P], BF16)
        select = sb("select", [P, PAIRS * P], F32R)
        band_bf = sb("band_bf", [P, NB * KW], BF16)
        table_probe = sb("table_probe", [P, 1])
        minus_half = sb("minus_half", [P, TILES])
        wq_sb, wk_sb, wv_sb, wo_sb = (sb(n, [P, P]) for n in ("wq_sb", "wk_sb", "wv_sb", "wo_sb"))
        bq_sb, bk_sb, bv_sb = (sb(n, [P, 1]) for n in ("bq_sb", "bk_sb", "bv_sb"))
        bv_wide, bo_wide, out_bias = (sb(n, [P, P]) for n in ("bv_wide", "bo_wide", "out_bias"))
        ones_bf, bias_part = sb("ones_bf", [P, P], BF16), sb("bias_part", [P, P], BF16)
        bias_parts = sb("bias_parts", [P, TILES, P], BF16)
        cls_sb, cls_t = sb("cls_sb", [EXPERTS, P]), sb("cls_t", [P, EXPERTS])
        cls_bias_sb = sb("cls_bias_sb", [P, EXPERTS])
        gu_hi, gu_lo = (sb(n, [P, PAIRS, 2, P], F32R) for n in ("gu_hi", "gu_lo"))
        down_hi, down_lo = (sb(n, [P, PAIRS, P], F32R) for n in ("down_hi", "down_lo"))

        x_sb = sb("x_sb", [P, TILES, P])
        WIDE = TILES * P
        carry_kept = sb("carry_kept", [P, 2, 2 * WIDE + TILES])
        carry, kept = carry_kept[:, 0], carry_kept[:, 1]

        def tiles(t):
            return t.rearrange("p (j h) -> p j h", j=TILES)

        x1, zero_part, x1_excess = tiles(carry[:, 0:WIDE]), tiles(carry[:, WIDE:2 * WIDE]), carry[:, 2 * WIDE:]
        x1_kept, zero_kept, excess_kept = tiles(kept[:, 0:WIDE]), tiles(kept[:, WIDE:2 * WIDE]), kept[:, 2 * WIDE:]
        x_stats, a_stats, y_stats = (sb(n, [P, TILES, 6]) for n in ("x_stats", "a_stats", "y_stats"))
        x_moments, a_moments, y_moments = (sb(n, [P, TILES, 2]) for n in ("x_moments", "a_moments", "y_moments"))
        x_var, x_neg, x_rstd, x_shift, a_var, a_rstd, y_var, y_neg, y_rstd, y_part, y_shift = (
            sb(n, [P, TILES]) for n in ("x_var", "x_neg", "x_rstd", "x_shift", "a_var", "a_rstd", "y_var", "y_neg",
                                        "y_rstd", "y_part", "y_shift"))
        xn_t = sb("xn_t", [P, SK])
        q_f, k_f = sb("q_f", [P, S]), sb("k_f", [P, S])
        qk_split = sb("qk_split", [P, 4, SK], F16)
        q_lo, q_hi, k_hi, k_lo = (qk_split[:, i, 0:S] if i < 2 else qk_split[:, i, PAD:PAD + S] for i in range(4))
        qk_parts = sb("qk_parts", [PARTS * QB, 2, HG, SK], F16)
        PART_PAIRS = (slice(1, 3), slice(1, 4, 2), slice(0, 3, 2))
        q_own = sb("q_own", [PARTS * QB, HG, NB, HPG, QB], F16)
        v_rows = sb("v_rows", [P, TILES + 1, HEADS, HC])
        v_own = sb("v_own", [P, NC, HPG, HG * HC])
        row_max = sb("row_max", [P, 2, HALF])
        probs = sb("probs", [P, NSTAGE, 2 * HALF * KW])
        probs_t = sb("probs_t", [P, 2, HG, HALF * KW])
        denom_inv = sb("denom_inv", [P, 2, HT * HEADS])
        heads_out, heads_t = sb("heads_out", [P, TILES, P]), sb("heads_t", [P, S])
        x_again = heads_out
        x2, x2_t = sb("x2", [P, TILES, P]), heads_t
        xn = x2
        x2_hi, x2_lo = sb("x2_hi", [P, S], F32R), sb("x2_lo", [P, S], F32R)
        r_max, r_sum, r_inv, zero_w = (sb(n, [P, TILES]) for n in ("r_max", "r_sum", "r_inv", "zero_w"))
        r_shift, r_exp, r_score, r_scaled, r_weight = (
            sb(n, [P, TILES, EXPERTS]) for n in ("r_shift", "r_exp", "r_score", "r_scaled", "r_weight"))
        r_biased, r_marked = (sb(n, [P, TILES, EXPERTS + 2]) for n in ("r_biased", "r_marked"))
        top8 = sb("top8", [P, TILES, 8])
        route_hl = sb("route_hl", [P, TILES, P], F32R)
        route_t = sb("route_t", [P, S], F32R)
        pair_sb = sb("pair_sb", [P, 3, 2, S])
        silu_sb, gated, hidden = pair_sb[:, 0], pair_sb[:, 1], pair_sb[:, 2]
        h_hi, h_lo = sb("h_hi", [P, HB, S], F32R), sb("h_lo", [P, HB, S], F32R)
        y_t = k_f
        tail_sb = sb("tail_sb", [P, 2, TILES, P])
        ffn, ffn_n = tail_sb[:, 0], tail_sb[:, 1]
        res = ffn

        pair_flat = pair_sb[:].rearrange("p a b c -> p (a b c)")
        HP = PAIRS // 2
        gu_rows = [pair_flat[:, 0:PAIRS * P].rearrange("p (a s m) -> p a s m", s=2, m=P),
                   carry_kept[:].rearrange("p c w -> p (c w)")[:, 0:PAIRS * P].rearrange(
                       "p (a s m) -> p a s m", s=2, m=P)]
        down_rows = [pair_flat[:, PAIRS * P:PAIRS * P + HP * P].rearrange("p (a m) -> p a m", m=P),
                     tail_sb[:].rearrange("p a j m -> p (a j) m")]

        x_in, x_again_in, table_in, front_in, back_in, gu_in, down_in, band_in, select_in, kept_in, out_done = map(sem, (
            "x_in", "x_again_in", "table_in", "front_in", "back_in", "gu_in", "down_in", "band_in", "select_in", "kept_in",
            "out_done"))
        pool_consts = sem("pool_consts")
        dve_consts = sem("dve_consts")
        bias_wide, setup_pe, setup_done = map(sem, ("bias_wide", "setup_pe", "setup_done"))
        turned, turned_hi, turned_lo = map(sem, ("turned", "turned_hi", "turned_lo"))
        work_b_free = sem("work_b_free")
        dve_step, pool_step = sem("dve_step"), sem("pool_step")
        x_moments_ready, x_rstd_ready, xn_ready, xn_turned, xn_t_ready, q_done, k_done, v_done = map(sem, (
            "x_moments_ready", "x_rstd_ready", "xn_ready", "xn_turned", "xn_t_ready", "q_done", "k_done", "v_done"))
        q_hi_ready, k_hi_ready, q_lo_ready, k_lo_ready, q_own_ready = map(sem, (
            "q_hi_ready", "k_hi_ready", "q_lo_ready", "k_lo_ready", "q_own_ready"))
        qk_parts_in = [sem(f"qk_parts_in_{gp}") for gp in range(2)]
        v_rows_ready, v_own_in, scores_done, shifted_ready, probs_ready = map(sem, (
            "v_rows_ready", "v_own_in", "scores_done", "shifted_ready", "probs_ready"))
        probs_t_ready = [sem(f"probs_t_ready_{hf}") for hf in range(2)]
        pv_done, heads_ready, heads_turned, heads_t_ready, attn_done = map(sem, (
            "pv_done", "heads_ready", "heads_turned", "heads_t_ready", "attn_done"))
        attn_var_ready, x1_var_ready, attn_rstd_ready, excess_ready, x1_rstd_ready, x2_ready = map(sem, (
            "attn_var_ready", "x1_var_ready", "attn_rstd_ready", "excess_ready", "x1_rstd_ready", "x2_ready"))
        x2_turned, x2_t_ready, x2_hi_ready, x2_lo_ready = map(sem, (
            "x2_turned", "x2_t_ready", "x2_hi_ready", "x2_lo_ready"))
        logits_done, r_shift_ready, r_exp_ready, zero_w_ready, route_ready, route_turned, route_t_ready = map(sem, (
            "logits_done", "r_shift_ready", "r_exp_ready", "zero_w_ready", "route_ready", "route_turned",
            "route_t_ready"))
        gate_done, up_done, route_wide, silu_ready, gated_ready, hidden_ready = map(sem, (
            "gate_done", "up_done", "route_wide", "silu_ready", "gated_ready", "hidden_ready"))
        h_hi_ready, h_lo_ready, down_done = map(sem, ("h_hi_ready", "h_lo_ready", "down_done"))
        y_t_ready, y_turned, zero_part_ready, y_moments_ready, y_rstd_ready, ffn_n_ready, res_ready = map(sem, (
            "y_t_ready", "y_turned", "zero_part_ready", "y_moments_ready", "y_rstd_ready", "ffn_n_ready", "res_ready"))

        def turn_target(n, gu, down):
            if n < GU_TURNS:
                return gu[:, 2 * n:2 * n + 2].rearrange("p a s m -> p (a s m)")
            n -= GU_TURNS
            return down[:, 4 * n:4 * n + 4].rearrange("p a m -> p (a m)")

        def at_least(eng, signal, count):
            if not (isinstance(count, int) and count <= 0):
                eng.wait_ge(signal, count)

        SLOTS = [*LATE, *EARLY]
        TURNED_AT = {-4: range(0, 3), -3: range(3, 6), -2: range(6, 8), 7: range(8, 12)}
        PE_AT = dict(mix_second=(-8, 2), turn_heads=(-7, 2), project=(-6, 0), turn_xn=(-6, 2), queries_keys=(-5, 1),
                     turn_x2=(-3, 0), logits=(-3, 1), values=(-1, 0), turn_route=(-1, 2),
                     scores=((1, 1), (2, 2), (3, 2), (4, 2)), turn_y=(4, 0), mix_first=(7, 1))
        ACT_AT = dict(take_heads=(-7, 1), first_norm=(-7, 2), take_xn=(-6, 2), queries=(-5, 2), keys=(-4, 1),
                      take_x2=(-3, 0), route_exp=(-2, 0), values=(-1, 0), take_route=(-1, 2), take_y=(2, 0),
                      exps=((3, 1), (4, 0), (6, 0), (6, 0)), tail_norm=(7, 0))
        DVE_AT = dict(divide=(-8, 2), first_statistics=(-8, 2), attention_statistics=(-6, 0), add_attention=(-5, 0),
                      second_norm=(-5, 2), route_shift=(-3, 1), route_scores=(-2, 0), find_top=(-2, 0),
                      weigh_experts=(-1, 0), queries_01=(-1, 1), queries_23=(0, 1),
                      shifts=((1, 1), (2, 2), (3, 2), (5, 0)), queries_23_first=(1, 2), tail_statistics=(4, 0),
                      probs=((5, 2), (6, 2), (6, 0), (7, 0)))
        POOL_AT = dict(first_deviations=(-7, 0), attention_deviations=(-7, 2), second_deviations=(-5, 2),
                       low_queries=(-4, 0), low_keys=(-4, 2), zero_experts=(1, 2), tail_deviations=(4, 2),
                       tail_residual=(7, 0))

        def first(a):
            return isinstance(a, int) and a == 0

        def pair_of(slot, late, early):
            return (late, slot + PAIRS) if slot < 0 else (early, slot)

        def run_steps(eng, step):
            step(0, None, None, None)
            step(1, 0, None, 0)
            with eng.Fori(2, NSEQ) as a:
                step(a, a - 1, a - 2, a - 1)
            step(None, NSEQ - 1, NSEQ - 2, NSEQ - 1)
            step(None, None, NSEQ - 1, None)

        block = ctx.enter_context(nc.Block())

        @block.sync
        def _(sp):
            def load_x(a):
                at_least(sp, xn_ready, TILES * a)
                sp.dma_start(x_sb[:], x[bass.ds(a, 1)].rearrange("a (j p) h -> p (a j) h", p=P)).then_inc(x_in, 16)

            def part_queries_keys(a):
                sp.wait_ge(q_lo_ready, a + 1)
                sp.wait_ge(k_lo_ready, a + 1)
                for g in range(HG):
                    for part, pair in enumerate(PART_PAIRS):
                        rows = slice(QB * g, QB * (g + 1))
                        sp.dma_start(qk_parts[QB * part:QB * (part + 1), :, g, :],
                                     qk_split[rows, pair, :]).then_inc(qk_parts_in[g // 2], 16)

            def spread_values(a):
                sp.wait_ge(v_rows_ready, 2 * (a + 1))
                for c in range(4):
                    rows, n = slice(QB * c, QB * (c + 1)), len(range(c, NC, 4))
                    for h in range(HPG):
                        sp.dma_start(v_own[QB * h:QB * (h + 1), c:NC:4, h, :],
                                     v_rows[rows, 0:n, HG * h:HG * (h + 1), :].rearrange("k n g d -> k n (g d)")
                                     ).then_inc(v_own_in, 16)

            def load_x_again(a):
                sp.wait_ge(heads_turned, a + 1)
                sp.dma_start(x_again[:],
                             x[bass.ds(a, 1)].rearrange("a (j p) h -> p (a j) h", p=P)).then_inc(x_again_in, 16)

            def store(e):
                sp.wait_ge(res_ready, e + 1)
                sp.dma_start(out[bass.ds(e, 1)].rearrange("a (j p) h -> p (a j) h", p=P), res).then_inc(out_done, 16)

            def keep(b):
                at_least(sp, res_ready, b)
                sp.wait_ge(zero_part_ready, b + 1)
                sp.dma_start(kept, carry).then_inc(kept_in, 16)

            load_x(0)
            sp.dma_start(table_sb[:], table).then_inc(table_in, 16)
            for dst, src in ((wq_sb, Wq), (wk_sb, Wk)):
                sp.dma_start(dst[:], src).then_inc(front_in, 16)
            gu = w_gu[0:ROUTED].rearrange("(p e) (s i) h -> e i p s h", e=2, s=2)
            down = w_down.rearrange("e h i -> h e i")
            for half in range(2):
                pairs = slice(HP * half, HP * (half + 1))
                for e in range(2):
                    for s in range(2):
                        sp.dma_start(gu_rows[half][INNER * e:INNER * (e + 1), :, s, :],
                                     gu[e, :, pairs, s, :]).then_inc(gu_in, 16)
                sp.dma_start(down_rows[half].rearrange("h p (e i) -> h (p e) i", e=2),
                             down[:, 2 * HP * half:2 * HP * (half + 1), :]).then_inc(down_in, 16)
            for dst, src in ((wo_sb, Wo), (bv_sb, bv.rearrange("(p a) -> p a", a=1)), (cls_sb, cls_w),
                             (bo_wide, bo.partition_broadcast(P)), (cls_bias_sb, cls_bias.partition_broadcast(P))):
                sp.dma_start(dst[:], src).then_inc(back_in, 16)
            part_queries_keys(0)
            sp.wait_ge(dve_consts, DVE_SETS)
            spread_values(0)
            load_x(1)
            load_x_again(0)
            part_queries_keys(1)
            spread_values(1)
            keep(0)
            with sp.Fori(2, NSEQ) as a:
                load_x(a)
                load_x_again(a - 1)
                part_queries_keys(a)
                spread_values(a)
                store(a - 2)
                keep(a - 1)
            load_x_again(NSEQ - 1)
            store(NSEQ - 2)
            keep(NSEQ - 1)
            store(NSEQ - 1)
            sp.wait_ge(out_done, 16 * (NSEQ + 1))

        @block.gpsimd
        def _(pool):
            pool.dma_start(band_bf[:], band).then_inc(band_in, 16)
            sets = [(minus_half[:], -0.5), (ones_bf[:], 1.0), (bias_parts[:], 0.0), (xn_t[:, 0:PAD], 0.0),
                    (xn_t[:, PAD + S:], 0.0), (qk_split[:, 0:2, S:], 0.0), (qk_split[:, 2:4, 0:PAD], 0.0),
                    (qk_split[:, 2:4, PAD + S:], 0.0), (r_biased[:], SENTINEL),
                    (route_hl[:, :, 2 * ROUTED:].bitcast(F32), 0.0)]
            assert len(sets) == POOL_SETS
            for dst, value in sets:
                pool.memset(dst, value).then_inc(pool_consts, 1)
            pool.dma_start(select[:], selector).then_inc(select_in, 16)
            pool.wait_ge(pool_consts, POOL_SETS)
            steps = [0]

            def ordered(ins):
                steps[0] += 1
                ins.then_inc(pool_step, 1)
                pool.wait_ge(pool_step, steps[0])

            def inverse_deviation(v, neg, r, sh):
                ordered(pool.tensor_tensor(r[:], v[:], minus_half[:], ALU.pow))
                return pool.tensor_tensor(sh[:], neg[:], r[:], ALU.mult)

            def first_deviations(a):
                pool.wait_ge(x_moments_ready, a + 1)
                inverse_deviation(x_var, x_neg, x_rstd, x_shift).then_inc(x_rstd_ready, 1)

            def attention_deviations(b):
                pool.wait_ge(attn_var_ready, b + 1)
                pool.tensor_tensor(a_rstd[:], a_var[:], minus_half[:], ALU.pow).then_inc(attn_rstd_ready, 1)
                pool.wait_ge(attn_rstd_ready, b + 1)
                at_least(pool, kept_in, 16 * b)
                pool.tensor_tensor(x1_excess, a_moments[:, :, 0], a_rstd[:], ALU.mult).then_inc(excess_ready, 1)

            def second_deviations(b):
                pool.wait_ge(x1_var_ready, b + 1)
                pool.tensor_tensor(a_rstd[:], a_var[:], minus_half[:], ALU.pow).then_inc(x1_rstd_ready, 1)

            def low_queries(a):
                pool.wait_ge(q_hi_ready, a + 1)
                pool.tensor_tensor(q_lo, q_f[:], q_hi, ALU.subtract).then_inc(q_lo_ready, 1)

            def low_keys(a):
                pool.wait_ge(k_hi_ready, a + 1)
                pool.tensor_tensor(k_lo, k_f[:], k_hi, ALU.subtract).then_inc(k_lo_ready, 1)

            def zero_experts(b):
                pool.wait_ge(zero_w_ready, b + 1)
                at_least(pool, kept_in, 16 * b)
                pool.tensor_tensor(zero_part, x2[:],
                                   zero_w[:].unsqueeze(2).broadcast_to([P, TILES, P]),
                                   ALU.mult).then_inc(zero_part_ready, 1)

            def hidden_low(e, p):
                n = e * PAIRS + p
                pool.wait_ge(h_hi_ready, n + 1)
                at_least(pool, down_done, n + 1 - HB)
                pool.tensor_tensor(h_lo[:, p % HB, :], hidden[:, p % 2, :], h_hi[:, p % HB, :].bitcast(F32),
                                   ALU.subtract).then_inc(h_lo_ready, 1)

            def tail_deviations(e):
                pool.wait_ge(y_moments_ready, e + 1)
                ordered(inverse_deviation(y_var, y_neg, y_rstd, y_part))
                pool.tensor_tensor(y_shift[:], y_part[:], excess_kept, ALU.subtract).then_inc(y_rstd_ready, 1)

            def tail_residual(e):
                pool.wait_ge(ffn_n_ready, TILES * (e + 1))
                pool.tensor_tensor(res, x1_kept, ffn_n, ALU.add).then_inc(res_ready, 1)

            def step(a, b, late, early):
                steps[0] = 0
                pool.sem_clear(pool_step)
                for slot in SLOTS:
                    for phase in (0, 2):
                        at = slot, phase
                        e, p = pair_of(slot - 1, late, early)
                        if phase == 2 and e is not None:
                            hidden_low(e, p)
                        if a is not None and at == POOL_AT["first_deviations"]:
                            first_deviations(a)
                        if b is not None:
                            if at == POOL_AT["attention_deviations"]:
                                attention_deviations(b)
                            if at == POOL_AT["second_deviations"]:
                                second_deviations(b)
                        if a is not None:
                            if at == POOL_AT["low_queries"]:
                                low_queries(a)
                            if at == POOL_AT["low_keys"]:
                                low_keys(a)
                        if b is not None and at == POOL_AT["zero_experts"]:
                            zero_experts(b)
                        if late is not None:
                            if at == POOL_AT["tail_deviations"]:
                                tail_deviations(late)
                            if at == POOL_AT["tail_residual"]:
                                tail_residual(late)

            run_steps(pool, step)

        @block.scalar
        def _(act):
            for dst, src in ((wv_sb, Wv), (bq_sb, bq.rearrange("(p a) -> p a", a=1)),
                             (bk_sb, bk.rearrange("(p a) -> p a", a=1))):
                act.dma_start(dst[:], src).then_inc(front_in, 16)

            def turned_high(n):
                if 0 <= n < TURNS:
                    act.wait_ge(turned, n + 1)
                    act.activation(turn_target(n, gu_hi, down_hi), turn_ps[n % 4][:], ACT.Copy).then_inc(turned_hi, 1)

            def normalise(dst, src, r, sh, signal):
                for j in range(TILES):
                    act.activation(dst[:, j, :], src(j), ACT.Identity, bias=sh[:, j:j + 1],
                                   scale=r[:, j:j + 1]).then_inc(signal, 1)

            def first_norm(a):
                act.wait_ge(x_rstd_ready, a + 1)
                normalise(xn, lambda j: x_sb[:, j, :], x_rstd, x_shift, xn_ready)

            def take_xn(a):
                act.wait_ge(xn_turned, a + 1)
                act.activation(xn_t[:, PAD:PAD + S], work_a[:], ACT.Copy).then_inc(xn_t_ready, 1)

            def queries(a):
                act.wait_ge(q_done, a + 1)
                if first(a):
                    act.wait_ge(front_in, 16 * FRONT)
                    act.wait_ge(pool_consts, POOL_SETS)
                act.activation(q_hi, work_b[:], ACT.Identity, bias=bq_sb[:, 0:1])
                act.activation(q_f[:], work_b[:], ACT.Identity, bias=bq_sb[:, 0:1]).then_inc(q_hi_ready, 1)

            def keys(a):
                act.wait_ge(k_done, a + 1)
                act.activation(k_hi, work_a[:], ACT.Identity, bias=bk_sb[:, 0:1])
                act.activation(k_f[:], work_a[:], ACT.Identity, bias=bk_sb[:, 0:1]).then_inc(k_hi_ready, 1)

            def values(a):
                act.wait_ge(v_done, a + 1)
                if first(a):
                    act.wait_ge(dve_consts, 1)
                act.activation(v_rows[:, 0:TILES, :, 0:HD],
                               score_ps[:, 0, :].rearrange("p (j h d) -> p j h d", h=HEADS, d=HD),
                               ACT.Copy).then_inc(v_rows_ready, 1)
                act.activation(v_rows[0:QB, TILES, :, 0:HD],
                               score_ps[0:QB, 1, 0:P].rearrange("p (h d) -> p h d", d=HD),
                               ACT.Copy).then_inc(v_rows_ready, 1)

            def exponentials(s, u):
                n = s * NSTAGE + u
                act.wait_ge(shifted_ready, 2 * (n + 1))
                act.activation(probs[:, u, :], probs[:, u, :], ACT.Exp, scale=scale).then_inc(probs_ready, 1)

            def take_heads(b):
                act.wait_ge(heads_turned, b + 1)
                act.activation(heads_t[:], score_ps[:, 0, :], ACT.Copy).then_inc(heads_t_ready, 1)

            def take_x2(b):
                act.wait_ge(x2_turned, b + 1)
                act.activation(x2_t[:], score_ps[:, 0, :], ACT.Copy).then_inc(x2_t_ready, 1)

            def route_exp(b):
                act.wait_ge(r_shift_ready, b + 1)
                act.activation(r_exp[:], r_shift[:], ACT.Exp).then_inc(r_exp_ready, 1)

            def high_x2(b):
                act.wait_ge(x2_t_ready, b + 1)
                at_least(act, up_done, b * PAIRS)
                act.activation(x2_hi[:], x2_t[:], ACT.Copy).then_inc(x2_hi_ready, 1)

            def take_route(b):
                act.wait_ge(route_turned, b + 1)
                at_least(act, route_wide, b * PAIRS)
                act.activation(route_t[:], score_ps[:, 0, :], ACT.Copy).then_inc(route_t_ready, 1)

            def silu(e, p):
                n = e * PAIRS + p
                act.wait_ge(gate_done, n + 1)
                at_least(act, gated_ready, n - 1)
                act.activation(silu_sb[:, p % 2, :], gate_ps[:], ACT.Silu).then_inc(silu_ready, 1)

            def hidden_high(e, p):
                n = e * PAIRS + p
                act.wait_ge(hidden_ready, n + 1)
                at_least(act, down_done, n + 1 - HB)
                act.activation(h_hi[:, p % HB, :], hidden[:, p % 2, :], ACT.Copy).then_inc(h_hi_ready, 1)

            def take_y(e, a):
                act.wait_ge(down_done, (e + 1) * PAIRS)
                if a is not None:
                    act.wait_ge(k_lo_ready, a + 1)
                act.activation(y_t[:], y_ps[:], ACT.Copy).then_inc(y_t_ready, 1)

            def tail_norm(e):
                act.wait_ge(y_rstd_ready, e + 1)
                normalise(ffn_n, lambda j: ffn[:, j, :], y_rstd, y_shift, ffn_n_ready)

            def step(a, b, late, early):
                for slot in SLOTS:
                    for phase in range(3):
                        at = slot, phase
                        if phase == 1:
                            e, p = pair_of(slot, late, early)
                            if e is not None:
                                silu(e, p)
                            if b is not None and slot == (-1 if late is not None else -3):
                                high_x2(b)
                        if phase == 2:
                            e, p = pair_of(slot - 1, late, early)
                            if e is not None:
                                hidden_high(e, p)
                        if a is not None and at == ACT_AT["first_norm"]:
                            first_norm(a)
                        if b is not None:
                            if at == ACT_AT["take_heads"]:
                                take_heads(b)
                            if at == ACT_AT["take_x2"]:
                                take_x2(b)
                            if at == ACT_AT["route_exp"]:
                                route_exp(b)
                                if late is None:
                                    act.activation(table_probe[:], minus_half[:, 0:1], ACT.Silu)
                            if at == ((0, 2) if late is None else ACT_AT["take_route"]):
                                take_route(b)
                        if a is not None:
                            if at == ACT_AT["take_xn"]:
                                take_xn(a)
                            if at == ACT_AT["queries"]:
                                queries(a)
                            if at == ACT_AT["keys"]:
                                keys(a)
                            if at == ACT_AT["values"]:
                                values(a)
                            for u in range(NSTAGE):
                                if at == ACT_AT["exps"][u]:
                                    exponentials(a, u)
                        if late is not None:
                            if at == ACT_AT["take_y"]:
                                take_y(late, a)
                            if at == ACT_AT["tail_norm"]:
                                tail_norm(late)
                    if a is not None and b is None:
                        for n in TURNED_AT.get(slot, ()):
                            turned_high(n)

            act.wait_ge(pool_consts, 1)
            act.activation(table_probe[:], minus_half[:, 0:1], ACT.Exp)
            run_steps(act, step)

        @block.vector
        def _(dve):
            steps = [0]

            def ordered(ins):
                steps[0] += 1
                ins.then_inc(dve_step, 1)
                dve.wait_ge(dve_step, steps[0])

            def turned_low(n):
                if 0 <= n < TURNS:
                    dve.wait_ge(turned_hi, n + 1)
                    dve.tensor_tensor(turn_target(n, gu_lo, down_lo), turn_ps[n % 4][:],
                                      turn_target(n, gu_hi, down_hi).bitcast(F32),
                                      ALU.subtract).then_inc(turned_lo, 1)

            def statistics(st, m, tile):
                for j in range(TILES):
                    last = dve.bn_stats(st[:, j, :], tile(j))
                ordered(last)
                for j in range(TILES):
                    last = dve.bn_aggr(m[:, j, :], st[:, j, :])
                return last

            def with_eps(v, m):
                return dve.tensor_scalar(v[:], m[:, :, 1], EPS, None, ALU.add)

            def negative_mean(neg, m):
                return dve.tensor_scalar(neg[:], m[:, :, 0], -1.0, None, ALU.mult)

            def normalise(dst, src, m):
                for j in range(TILES):
                    last = dve.tensor_scalar(dst[:, j, :], src[:, j, :], m[:, j, 0:1], a_rstd[:, j:j + 1],
                                             ALU.subtract, ALU.mult)
                return last

            def first_statistics(a):
                dve.wait_ge(x_in, 16 * (a + 1))
                ordered(statistics(x_stats, x_moments, lambda j: x_sb[:, j, :]))
                with_eps(x_var, x_moments)
                negative_mean(x_neg, x_moments).then_inc(x_moments_ready, 1)

            def own_queries(a, gp):
                dve.wait_ge(qk_parts_in[gp], 16 * PARTS * 2 * (a + 1))
                for h in range(HPG):
                    dve.tensor_scalar(q_own[:, 2 * gp:2 * gp + 2, :, h, :],
                                      qk_parts[:, 0, 2 * gp:2 * gp + 2, 0:S].rearrange("p g (b q) -> p g b q", q=QB),
                                      own_head[0:PARTS * QB, h:h + 1], None, ALU.mult).then_inc(q_own_ready, 1)

            def shift_scores(s, u):
                n = s * NSTAGE + u
                def found(i):
                    return score_ps[:, i, :].rearrange("p (b k) -> p b k", b=HALF)
                for i in range(2):
                    dve.wait_ge(scores_done, 2 * n + i + 1)
                    last = dve.tensor_reduce(row_max[:, i], found(i), AX_X, ALU.max)
                ordered(last)
                at_least(dve, probs_t_ready[STAGES[u][0]], 2 * s)
                for i in range(2):
                    below = probs[:, u, i * HALF * KW:(i + 1) * HALF * KW].rearrange("p (b k) -> p b k", b=HALF)
                    dve.tensor_tensor(below, found(i), row_max[:, i].unsqueeze(2).broadcast_to([P, HALF, KW]),
                                      ALU.subtract).then_inc(shifted_ready, 1)

            def turn_probs(s, u):
                hf, gp = STAGES[u]
                dve.wait_ge(probs_ready, s * NSTAGE + u + 1)
                dve.transpose(probs_t[:, hf, 2 * gp:2 * gp + 2, :],
                              probs[:, u, :].rearrange("p (g c) -> p g c", g=2)).then_inc(probs_t_ready[hf], 1)

            def divide_heads(s, hf):
                dve.wait_ge(pv_done, 2 * s + hf + 1)
                sums = (work_a, work_b)[hf][:, 0:HT * HEADS * HC].rearrange("p (a c) -> p a c", c=HC)
                ordered(dve.reciprocal(denom_inv[:, hf, :], sums[:, :, HD]))
                dve.tensor_tensor(heads_out[:, HT * hf:HT * (hf + 1), :].rearrange("p j (a d) -> p (j a) d", d=HD),
                                  sums[:, :, 0:HD], denom_inv[:, hf, :].unsqueeze(2).broadcast_to([P, HT * HEADS, HD]),
                                  ALU.mult).then_inc(heads_ready, 1)

            def attention_statistics(b):
                dve.wait_ge(attn_done, b + 1)
                ordered(statistics(a_stats, a_moments, lambda j: score_ps[:, 1, P * j:P * (j + 1)]))
                with_eps(a_var, a_moments).then_inc(attn_var_ready, 1)

            def add_attention(b):
                dve.wait_ge(attn_rstd_ready, b + 1)
                dve.wait_ge(x_again_in, 16 * (b + 1))
                at_least(dve, kept_in, 16 * b)
                for j in range(TILES):
                    last = dve.scalar_tensor_tensor(out=x1[:, j, :], in0=score_ps[:, 1, P * j:P * (j + 1)],
                                                    scalar=a_rstd[:, j:j + 1], in1=x_again[:, j, :],
                                                    op0=ALU.mult, op1=ALU.add)
                ordered(last)
                dve.wait_ge(excess_ready, b + 1)
                ordered(statistics(a_stats, a_moments, lambda j: x1[:, j, :]))
                with_eps(a_var, a_moments).then_inc(x1_var_ready, 1)

            def second_norm(b, a):
                dve.wait_ge(x1_rstd_ready, b + 1)
                if a is not None:
                    dve.wait_ge(xn_turned, a + 1)
                normalise(x2, x1, a_moments).then_inc(x2_ready, 1)

            def wide(t):
                return t[:].unsqueeze(2).broadcast_to([P, TILES, EXPERTS])

            def route_shift(s):
                dve.wait_ge(logits_done, s + 1)
                logits = score_ps[:, 1, 0:TILES * EXPERTS].rearrange("p (j e) -> p j e", j=TILES)
                ordered(dve.tensor_reduce(r_max[:], logits, AX_X, ALU.max))
                dve.tensor_tensor(r_shift[:], logits, wide(r_max), ALU.subtract).then_inc(r_shift_ready, 1)

            def route_scores(s):
                dve.wait_ge(r_exp_ready, s + 1)
                ordered(dve.tensor_reduce(r_sum[:], r_exp[:], AX_X, ALU.add))
                ordered(dve.reciprocal(r_inv[:], r_sum[:]))
                ordered(dve.tensor_tensor(r_score[:], r_exp[:], wide(r_inv), ALU.mult))
                dve.tensor_scalar(r_scaled[:], r_score[:], ROUTE_SCALE, None, ALU.mult)
                ordered(dve.tensor_tensor(r_biased[:, :, 0:EXPERTS], r_score[:],
                                          cls_bias_sb[:].unsqueeze(1).broadcast_to([P, TILES, EXPERTS]), ALU.add))

            def find_top(s):
                for j in range(TILES):
                    last = dve.max(top8[:, j, :], r_biased[:, j, 0:EXPERTS])
                ordered(last)
                ordered(dve.memset(top8[:, :, TOPK:8], SENTINEL))

            def weigh_experts(s):
                for j in range(TILES):
                    last = dve.match_replace(r_marked[:, j, :], top8[:, j, :], r_biased[:, j, :], TAKEN)
                ordered(last)
                ordered(dve.scalar_tensor_tensor(out=r_weight[:], in0=r_marked[:, :, 0:EXPERTS], scalar=TAKEN,
                                                 in1=r_scaled[:], op0=ALU.is_equal, op1=ALU.mult))
                dve.tensor_reduce(zero_w[:], r_weight[:, :, ROUTED:EXPERTS], AX_X, ALU.add).then_inc(zero_w_ready, 1)
                ordered(dve.tensor_copy(route_hl[:, :, 0:ROUTED], r_weight[:, :, 0:ROUTED]))
                dve.tensor_tensor(route_hl[:, :, ROUTED:2 * ROUTED], r_weight[:, :, 0:ROUTED],
                                  route_hl[:, :, 0:ROUTED].bitcast(F32), ALU.subtract).then_inc(route_ready, 1)

            def low_x2(s):
                dve.wait_ge(x2_hi_ready, s + 1)
                dve.tensor_tensor(x2_lo[:], x2_t[:], x2_hi[:].bitcast(F32), ALU.subtract).then_inc(x2_lo_ready, 1)

            def gate_up(e, p):
                n = e * PAIRS + p
                dve.wait_ge(silu_ready, n + 1)
                dve.wait_ge(up_done, n + 1)
                dve.tensor_tensor(gated[:, p % 2, :], silu_sb[:, p % 2, :], up_ps[:], ALU.mult).then_inc(gated_ready, 1)

            def weigh(e, p):
                n = e * PAIRS + p
                dve.wait_ge(gated_ready, n + 1)
                dve.wait_ge(route_wide, n + 1)
                at_least(dve, h_lo_ready, n - 1)
                dve.tensor_tensor(hidden[:, p % 2, :], gated[:, p % 2, :], route_ps[:],
                                  ALU.mult).then_inc(hidden_ready, 1)

            def tail_statistics(e):
                dve.wait_ge(y_turned, e + 1)
                dve.wait_ge(kept_in, 16 * (e + 1))
                dve.wait_ge(out_done, 16 * (e + 1))
                ordered(dve.tensor_tensor(ffn, work_b[:].rearrange("p (j h) -> p j h", j=TILES),
                                          zero_kept, ALU.add))
                ordered(statistics(y_stats, y_moments, lambda j: ffn[:, j, :]))
                with_eps(y_var, y_moments).then_inc(work_b_free, 1)
                negative_mean(y_neg, y_moments).then_inc(y_moments_ready, 1)

            def step(a, b, late, early):
                steps[0] = 0
                dve.sem_clear(dve_step)
                for slot in SLOTS:
                    for phase in range(3):
                        at = slot, phase
                        if phase == 1:
                            e, p = pair_of(slot, late, early)
                            if e is not None:
                                gate_up(e, p)
                            if b is not None and slot == (-1 if late is not None else -3):
                                low_x2(b)
                        if phase == 2:
                            e, p = pair_of(slot, late, early)
                            if e is not None:
                                weigh(e, p)
                        if b is not None:
                            if at == DVE_AT["divide"]:
                                divide_heads(b, 0)
                                divide_heads(b, 1)
                            if at == DVE_AT["attention_statistics"]:
                                attention_statistics(b)
                            if at == DVE_AT["add_attention"]:
                                add_attention(b)
                            if at == DVE_AT["second_norm"]:
                                second_norm(b, a)
                            if at == DVE_AT["route_shift"]:
                                route_shift(b)
                            if at == DVE_AT["route_scores"]:
                                route_scores(b)
                            if at == DVE_AT["find_top"]:
                                find_top(b)
                            if at == DVE_AT["weigh_experts"]:
                                weigh_experts(b)
                        if a is not None:
                            if at == DVE_AT["first_statistics"]:
                                first_statistics(a)
                            if at == DVE_AT["queries_01"]:
                                own_queries(a, 0)
                            for u in (0, 2, 1, 3):
                                if at == DVE_AT["probs"][u]:
                                    turn_probs(a, u)
                            for u in range(NSTAGE):
                                if at == DVE_AT["shifts"][u]:
                                    shift_scores(a, u)
                            if at == DVE_AT["queries_23_first" if first(a) else "queries_23"]:
                                own_queries(a, 1)
                        if late is not None and at == DVE_AT["tail_statistics"]:
                            tail_statistics(late)
                    if a is not None and b is None:
                        for n in TURNED_AT.get(slot, ()):
                            turned_low(n)
                        if slot == -8:
                            dve.memset(v_own[:], 0.0).then_inc(dve_consts, 1)
                        if slot == 4:
                            widen_bias()
                        if slot == 7:
                            output_bias()

            def widen_bias():
                dve.wait_ge(back_in, 16 * BACK)
                dve.tensor_copy(bv_wide[:], bv_sb[:, 0:1].broadcast_to([P, P])).then_inc(bias_wide, 1)

            def output_bias():
                dve.wait_ge(setup_pe, 1)
                dve.wait_ge(pool_consts, POOL_SETS)
                dve.tensor_copy(cls_t[:], score_ps[:, 1, 0:EXPERTS]).then_inc(setup_done, 1)
                ordered(dve.tensor_tensor(out_bias[:], score_ps[:, 0, 0:P], bo_wide[:], ALU.add))
                for row in (0, 32, 64):
                    ordered(dve.tensor_copy(bias_part[:], out_bias[:]))
                    dve.tensor_copy(bias_parts[row:row + 1], bias_part[row:row + 1].unsqueeze(1).broadcast_to(
                        [1, TILES, P])).then_inc(setup_done, 1)
                    ordered(dve.tensor_tensor(out_bias[:], out_bias[:], bias_part[:], ALU.subtract))

            dve.memset(v_rows[:], 1.0).then_inc(dve_consts, 1)
            dve.memset(y_part[:], 0.0).then_inc(work_b_free, 1)
            dve.memset(y_shift[:], 0.0).then_inc(out_done, 16)
            dve.wait_ge(table_in, 16)
            dve.tensor_copy(ident_bf[:], ident).then_inc(dve_consts, 1)
            run_steps(dve, step)

        @block.tensor
        def _(pe):
            def turn_weights(n):
                if not 0 <= n < TURNS:
                    return
                at_least(pe, turned_hi, n - 3)
                at_least(pe, turned_lo, n - 3)
                if n < GU_TURNS:
                    if n % (GU_TURNS // 2) == 0:
                        pe.wait_ge(gu_in, 128)
                    half, first = divmod(2 * n, HP)
                    tiles = [gu_rows[half][:, first + i // 2, i % 2, :] for i in range(4)]
                else:
                    pe.wait_ge(down_in, 32)
                    half, first = divmod(4 * (n - GU_TURNS), HP)
                    tiles = [down_rows[half][:, first + i, :] for i in range(4)]
                for i, t in enumerate(tiles):
                    last = pe.transpose(turn_ps[n % 4][:, P * i:P * (i + 1)], t, ident)
                last.then_inc(turned, 1)

            def turn_tiles(ps, src):
                for j in range(TILES):
                    last = pe.transpose(ps[:, P * j:P * (j + 1)], src[:, j, :], ident)
                return last

            def turn_xn(a):
                pe.wait_ge(xn_ready, TILES * (a + 1))
                at_least(pe, heads_ready, 2 * a)
                turn_tiles(work_a[:], xn).then_inc(xn_turned, 1)

            def queries_keys(a):
                pe.wait_ge(xn_t_ready, a + 1)
                if first(a):
                    pe.wait_ge(front_in, 16 * FRONT)
                    pe.wait_ge(pool_consts, POOL_SETS)
                pe.matmul(work_b[:], wq_sb[:], xn_t[:, PAD:PAD + S], start=True, stop=True).then_inc(q_done, 1)
                pe.matmul(work_a[:], wk_sb[:], xn_t[:, PAD:PAD + S], start=True, stop=True).then_inc(k_done, 1)

            def values(a):
                at_least(pe, r_shift_ready, a)
                for j in range(TILES + 1):
                    keys = min(P, SK - P * j)
                    last = pe.matmul(score_flat[0:keys, P * j:P * (j + 1)], xn_t[:, P * j:P * j + keys],
                                     wv_sb[:].rearrange("i (g h d) -> i h g d", g=HG, h=HPG), start=True, stop=True)
                last.then_inc(v_done, 1)

            def scores(a, u):
                hf, gp = STAGES[u]
                if hf == 0:
                    pe.wait_ge(q_own_ready, HPG * (2 * a + gp + 1))
                    pe.wait_ge(qk_parts_in[gp], 16 * PARTS * 2 * (a + 1))
                if u == 0:
                    if first(a):
                        pe.wait_ge(band_in, 16)
                        pe.wait_ge(dve_consts, 2)
                    pe.wait_ge(v_rows_ready, 2 * (a + 1))
                    at_least(pe, route_t_ready, a)
                for i in range(2):
                    if u > 0:
                        pe.wait_ge(shifted_ready, 2 * (a * NSTAGE + u - 1) + i + 1)
                    pe.matmul(score_ps[:, i, :], ident_bf[:], band_bf[:, hf * 512:(hf + 1) * 512],
                              start=True, stop=False, skip_group_check=True)
                    for b in range(HALF):
                        at = QB * (hf * HALF + b)
                        last = pe.matmul(score_ps[:, i, KW * b:KW * (b + 1)],
                                         q_own[:, 2 * gp + i, hf * HALF + b].rearrange("p h q -> p (h q)"),
                                         qk_parts[:, 1, 2 * gp + i, at:at + KW], start=False, stop=True,
                                         skip_group_check=True)
                    last.then_inc(scores_done, 1)

            def mix_values(s, hf):
                pe.wait_ge(probs_t_ready[hf], 2 * (s + 1))
                if hf == 0:
                    pe.wait_ge(v_own_in, 16 * 4 * HPG * (s + 1))
                else:
                    at_least(pe, work_b_free, s)
                for j in range(HT):
                    for g in range(HG):
                        col = (j * HG + g) * GW
                        for side in range(2):
                            for r in range(4):
                                b = 4 * j + r
                                last = pe.matmul((work_a, work_b)[hf][QB * r:QB * (r + 1), col:col + GW],
                                                 probs_t[:, hf, g, b * KW + side * QB:b * KW + (side + 1) * QB],
                                                 v_own[:, hf * HALF + b + side, :, HC * g:HC * (g + 1)],
                                                 start=(side == 0), stop=(side == 1), skip_group_check=True)
                last.then_inc(pv_done, 1)

            def turn_heads(b):
                pe.wait_ge(heads_ready, 2 * (b + 1))
                pe.wait_ge(shifted_ready, 2 * NSTAGE * (b + 1))
                turn_tiles(score_ps[:, 0, :], heads_out).then_inc(heads_turned, 1)

            def project_heads(b):
                if first(b):
                    pe.wait_ge(setup_done, 4)
                pe.matmul(score_ps[:, 1, :], ones_bf[:], bias_parts[:].rearrange("p j h -> p (j h)"), start=True,
                          stop=False, skip_group_check=True)
                pe.wait_ge(heads_t_ready, b + 1)
                for j in range(TILES):
                    last = pe.matmul(score_ps[:, 1, P * j:P * (j + 1)], heads_t[:, P * j:P * (j + 1)], wo_sb[:],
                                     start=False, stop=True, skip_group_check=True)
                last.then_inc(attn_done, 1)

            def turn_x2(b):
                pe.wait_ge(x2_ready, b + 1)
                turn_tiles(score_ps[:, 0, :], x2).then_inc(x2_turned, 1)

            def logits(b):
                pe.wait_ge(x2_t_ready, b + 1)
                for j in range(TILES):
                    last = pe.matmul(score_ps[:, 1, EXPERTS * j:EXPERTS * (j + 1)], x2_t[:, P * j:P * (j + 1)],
                                     cls_t[:], start=True, stop=True)
                last.then_inc(logits_done, 1)

            def turn_route(b, a):
                pe.wait_ge(route_ready, b + 1)
                if a is not None:
                    pe.wait_ge(v_rows_ready, 2 * (a + 1))
                for j in range(TILES):
                    last = pe.transpose(score_ps[:, 0, P * j:P * (j + 1)], route_hl[:, j, :].bitcast(F32), ident)
                last.then_inc(route_turned, 1)

            def three_products(ps, w_hi, w_lo, a_hi, a_lo, start, stop):
                pe.matmul(ps, w_hi, a_hi, start=start, stop=False)
                pe.matmul(ps, w_lo, a_hi, start=False, stop=False)
                return pe.matmul(ps, w_hi, a_lo, start=False, stop=stop)

            def gate_and_up(e, p):
                n = e * PAIRS + p
                if p == 0:
                    pe.wait_ge(x2_hi_ready, e + 1)
                    pe.wait_ge(x2_lo_ready, e + 1)
                at_least(pe, silu_ready, n)
                three_products(gate_ps[:], gu_hi[:, p, 0, :], gu_lo[:, p, 0, :], x2_hi[:], x2_lo[:],
                               True, True).then_inc(gate_done, 1)
                at_least(pe, gated_ready, n)
                three_products(up_ps[:], gu_hi[:, p, 1, :], gu_lo[:, p, 1, :], x2_hi[:], x2_lo[:],
                               True, True).then_inc(up_done, 1)

            def spread_route(e, p):
                n = e * PAIRS + p
                if p == 0:
                    pe.wait_ge(route_t_ready, e + 1)
                    if first(e):
                        pe.wait_ge(select_in, 16)
                at_least(pe, hidden_ready, n)
                pe.matmul(route_ps[:], select[:, P * p:P * (p + 1)], route_t[:], start=True,
                          stop=True).then_inc(route_wide, 1)

            def expert_down(e, p):
                n = e * PAIRS + p
                pe.wait_ge(h_hi_ready, n + 1)
                pe.wait_ge(h_lo_ready, n + 1)
                if p == 0:
                    at_least(pe, y_t_ready, e)
                three_products(y_ps[:], down_hi[:, p, :], down_lo[:, p, :], h_hi[:, p % HB, :], h_lo[:, p % HB, :],
                               p == 0, p == PAIRS - 1).then_inc(down_done, 1)

            def turn_y(e):
                pe.wait_ge(y_t_ready, e + 1)
                for j in range(TILES):
                    last = pe.transpose(work_b[:, P * j:P * (j + 1)], y_t[:, P * j:P * (j + 1)], ident)
                last.then_inc(y_turned, 1)

            def setup():
                pe.wait_ge(back_in, 16 * BACK)
                pe.wait_ge(bias_wide, 1)
                pe.wait_ge(shifted_ready, 2 * NSTAGE)
                pe.matmul(score_ps[:, 0, 0:P], bv_wide[:], wo_sb[:], start=True, stop=True)
                pe.transpose(score_ps[:, 1, 0:EXPERTS], cls_sb[:], ident[0:EXPERTS, 0:EXPERTS]).then_inc(setup_pe, 1)

            def step(a, b, late, early):
                for slot in SLOTS:
                    e, p = pair_of(slot - LAG, late, early)
                    if e is not None:
                        expert_down(e, p)
                    for phase in range(3):
                        at = slot, phase
                        e, p = pair_of(slot, late, early)
                        if e is not None and phase == 1:
                            gate_and_up(e, p)
                        if b is not None and at == ((0, 1) if late is None else PE_AT["turn_route"]):
                            turn_route(b, a)
                        if e is not None and phase == 2:
                            spread_route(e, p)
                        if b is not None:
                            if at == PE_AT["mix_second"]:
                                mix_values(b, 1)
                            if at == PE_AT["turn_heads"]:
                                turn_heads(b)
                            if at == PE_AT["project"]:
                                project_heads(b)
                            if at == PE_AT["turn_x2"]:
                                turn_x2(b)
                            if at == PE_AT["logits"]:
                                logits(b)
                        if a is not None:
                            if at == PE_AT["turn_xn"]:
                                turn_xn(a)
                            if at == PE_AT["queries_keys"]:
                                queries_keys(a)
                            if at == PE_AT["values"]:
                                values(a)
                            for u in range(NSTAGE):
                                if at == PE_AT["scores"][u]:
                                    scores(a, u)
                            if at == PE_AT["mix_first"]:
                                if b is None:
                                    for n in TURNED_AT[slot]:
                                        turn_weights(n)
                                mix_values(a, 0)
                        if late is not None and at == PE_AT["turn_y"]:
                            turn_y(late)
                    if a is not None and b is None:
                        if slot != PE_AT["mix_first"][0]:
                            for n in TURNED_AT.get(slot, ()):
                                turn_weights(n)
                        if slot == 7:
                            setup()

            pe.wait_ge(table_in, 16)
            run_steps(pe, step)


_INS = ["L0_attn_x", "L0_attn_Wq", "L0_attn_bq", "L0_attn_Wk", "L0_attn_bk", "L0_attn_Wv", "L0_attn_bv",
        "L0_attn_Wo", "L0_attn_bo", "L0_ffn_classifier_weight", "L0_ffn_e_score_correction_bias",
        "L0_ffn_gate_up_proj", "L0_ffn_down_proj"]


def kernel(**inputs):
    import concourse.bacc as bacc
    from concourse.bass_utils import run_bass_kernel_spmd

    nc = bacc.Bacc("TRN2", target_bir_lowering=False, num_devices=1)
    arrays = {f"in_{name}": np.ascontiguousarray(inputs[name]) for name in _INS}
    shape = inputs["L0_attn_x"].shape
    arrays["table"], arrays["band"], arrays["selector"] = shape_constants(shape[1])
    args = [nc.dram_tensor(name, a.shape, mybir.dt.from_np(a.dtype), kind="ExternalInput").ap()
            for name, a in arrays.items()]
    out = nc.dram_tensor("out", shape, F32, kind="ExternalOutput").ap()
    build_block(nc, *args, out)
    r = run_bass_kernel_spmd(nc, [arrays], core_ids=[0])
    return r.results[0]["out"]
```
